# Optimizing a Trainium2 kernel written in Bass

```python
import numpy as np
import jax
import jax.numpy as jnp

def _softmax(x, axis=-1):
    return jax.nn.softmax(x, axis=axis)

def _gelu(x):
    return jax.nn.gelu(x, approximate=True)

def _silu(x):
    return jax.nn.silu(x)

def _sigmoid(x):
    return jax.nn.sigmoid(x)

def _layernorm(x, axis=-1, eps=1e-05):
    m = jnp.mean(x, axis=axis, keepdims=True)
    v = jnp.var(x, axis=axis, keepdims=True)
    return (x - m) / jnp.sqrt(v + eps)

def _scatter_add(tgt, idx, src, axis=0):
    return tgt.at[idx].add(src)

def _segment_sum(src, seg, n):
    return jax.ops.segment_sum(src, seg, n)
kernel_name = 'mk_dlrm_tower_d1_rec_r8_cf4efc'

def setup_inputs(seed: int=0):
    np.random.seed(seed)
    _w = jnp.asarray

    def _rec_inputs():
        import jax
        import jax.numpy as jnp
        _tk = jax.random.key(seed)
        dense_ctx = jax.random.normal(jax.random.fold_in(_tk, 190), (512, 16), jnp.float32)
        ids = jnp.stack([jax.random.randint(jax.random.fold_in(_tk, 200 + f), (512,), 0, v, jnp.int32) for f, v in enumerate([1250, 12500, 1250, 1000, 125000, 1000, 12500, 1250, 12500, 12500, 1000, 1250, 125000, 12500, 125000, 1000, 125000, 1250, 12500, 125000, 125000, 12500, 1000, 1250, 125000, 1250, 1250, 1250, 1250, 1000, 1000, 1000])], axis=1)
        tbl_0 = 0.05 * jax.random.normal(jax.random.fold_in(_tk, 500 + 0), (1250, 32), jnp.float32)
        tbl_1 = 0.05 * jax.random.normal(jax.random.fold_in(_tk, 500 + 1), (12500, 32), jnp.float32)
        tbl_2 = 0.05 * jax.random.normal(jax.random.fold_in(_tk, 500 + 2), (1250, 32), jnp.float32)
        tbl_3 = 0.05 * jax.random.normal(jax.random.fold_in(_tk, 500 + 3), (1000, 32), jnp.float32)
        tbl_4 = 0.05 * jax.random.normal(jax.random.fold_in(_tk, 500 + 4), (125000, 32), jnp.float32)
        tbl_5 = 0.05 * jax.random.normal(jax.random.fold_in(_tk, 500 + 5), (1000, 32), jnp.float32)
        tbl_6 = 0.05 * jax.random.normal(jax.random.fold_in(_tk, 500 + 6), (12500, 32), jnp.float32)
        tbl_7 = 0.05 * jax.random.normal(jax.random.fold_in(_tk, 500 + 7), (1250, 32), jnp.float32)
        tbl_8 = 0.05 * jax.random.normal(jax.random.fold_in(_tk, 500 + 8), (12500, 32), jnp.float32)
        tbl_9 = 0.05 * jax.random.normal(jax.random.fold_in(_tk, 500 + 9), (12500, 32), jnp.float32)
        tbl_10 = 0.05 * jax.random.normal(jax.random.fold_in(_tk, 500 + 10), (1000, 32), jnp.float32)
        tbl_11 = 0.05 * jax.random.normal(jax.random.fold_in(_tk, 500 + 11), (1250, 32), jnp.float32)
        tbl_12 = 0.05 * jax.random.normal(jax.random.fold_in(_tk, 500 + 12), (125000, 32), jnp.float32)
        tbl_13 = 0.05 * jax.random.normal(jax.random.fold_in(_tk, 500 + 13), (12500, 32), jnp.float32)
        tbl_14 = 0.05 * jax.random.normal(jax.random.fold_in(_tk, 500 + 14), (125000, 32), jnp.float32)
        tbl_15 = 0.05 * jax.random.normal(jax.random.fold_in(_tk, 500 + 15), (1000, 32), jnp.float32)
        tbl_16 = 0.05 * jax.random.normal(jax.random.fold_in(_tk, 500 + 16), (125000, 32), jnp.float32)
        tbl_17 = 0.05 * jax.random.normal(jax.random.fold_in(_tk, 500 + 17), (1250, 32), jnp.float32)
        tbl_18 = 0.05 * jax.random.normal(jax.random.fold_in(_tk, 500 + 18), (12500, 32), jnp.float32)
        tbl_19 = 0.05 * jax.random.normal(jax.random.fold_in(_tk, 500 + 19), (125000, 32), jnp.float32)
        tbl_20 = 0.05 * jax.random.normal(jax.random.fold_in(_tk, 500 + 20), (125000, 32), jnp.float32)
        tbl_21 = 0.05 * jax.random.normal(jax.random.fold_in(_tk, 500 + 21), (12500, 32), jnp.float32)
        tbl_22 = 0.05 * jax.random.normal(jax.random.fold_in(_tk, 500 + 22), (1000, 32), jnp.float32)
        tbl_23 = 0.05 * jax.random.normal(jax.random.fold_in(_tk, 500 + 23), (1250, 32), jnp.float32)
        tbl_24 = 0.05 * jax.random.normal(jax.random.fold_in(_tk, 500 + 24), (125000, 32), jnp.float32)
        tbl_25 = 0.05 * jax.random.normal(jax.random.fold_in(_tk, 500 + 25), (1250, 32), jnp.float32)
        tbl_26 = 0.05 * jax.random.normal(jax.random.fold_in(_tk, 500 + 26), (1250, 32), jnp.float32)
        tbl_27 = 0.05 * jax.random.normal(jax.random.fold_in(_tk, 500 + 27), (1250, 32), jnp.float32)
        tbl_28 = 0.05 * jax.random.normal(jax.random.fold_in(_tk, 500 + 28), (1250, 32), jnp.float32)
        tbl_29 = 0.05 * jax.random.normal(jax.random.fold_in(_tk, 500 + 29), (1000, 32), jnp.float32)
        tbl_30 = 0.05 * jax.random.normal(jax.random.fold_in(_tk, 500 + 30), (1000, 32), jnp.float32)
        tbl_31 = 0.05 * jax.random.normal(jax.random.fold_in(_tk, 500 + 31), (1000, 32), jnp.float32)
        _rk = jax.random.fold_in(_tk, 7)
        W_top1 = 0.0606339 * jax.random.normal(jax.random.fold_in(_tk, 801), (272, 512), jnp.float32)
        W_top2 = 0.0441942 * jax.random.normal(jax.random.fold_in(_tk, 802), (512, 256), jnp.float32)
        W_top3 = 0.0625 * jax.random.normal(jax.random.fold_in(_tk, 803), (256, 1), jnp.float32)
        b_top1 = jnp.zeros((512,), jnp.float32)
        b_top2 = jnp.zeros((256,), jnp.float32)
        return (dense_ctx, ids, tbl_0, tbl_1, tbl_2, tbl_3, tbl_4, tbl_5, tbl_6, tbl_7, tbl_8, tbl_9, tbl_10, tbl_11, tbl_12, tbl_13, tbl_14, tbl_15, tbl_16, tbl_17, tbl_18, tbl_19, tbl_20, tbl_21, tbl_22, tbl_23, tbl_24, tbl_25, tbl_26, tbl_27, tbl_28, tbl_29, tbl_30, tbl_31, W_top1, b_top1, W_top2, b_top2, W_top3)
    dense_ctx, ids, tbl_0, tbl_1, tbl_2, tbl_3, tbl_4, tbl_5, tbl_6, tbl_7, tbl_8, tbl_9, tbl_10, tbl_11, tbl_12, tbl_13, tbl_14, tbl_15, tbl_16, tbl_17, tbl_18, tbl_19, tbl_20, tbl_21, tbl_22, tbl_23, tbl_24, tbl_25, tbl_26, tbl_27, tbl_28, tbl_29, tbl_30, tbl_31, W_top1, b_top1, W_top2, b_top2, W_top3 = _rec_inputs()

    def _L0_rec_setup():
        import jax, jax.numpy as jnp
        import numpy as np
        B, F, D = (512, 32, 32)
        LAYER_SIZE = [128, 128]

        def _cin_forward(inputs, filters):
            x0 = inputs
            prev = inputs
            outs = []
            for W in filters:
                z = jnp.einsum('bhd,bmd->bhmd', x0, prev)
                b, h, m, d = z.shape
                z = z.reshape(b, h * m, d)
                cur = jnp.einsum('bpd,pn->bnd', z, W[0])
                cur = jax.nn.relu(cur)
                prev = cur
                outs.append(cur)
            result = jnp.concatenate(outs, axis=1)
            return jnp.sum(result, axis=-1)
        key = jax.random.key(seed)
        k1, k2, k3 = jax.random.split(key, 3)
        inputs = jax.random.normal(k1, (B, F, D), dtype=jnp.float32)
        field_nums = [F] + LAYER_SIZE
        filter_0 = jax.random.normal(k2, (1, field_nums[0] * field_nums[0], field_nums[1]), dtype=jnp.float32) * 0.05
        filter_1 = jax.random.normal(k3, (1, field_nums[0] * field_nums[1], field_nums[2]), dtype=jnp.float32) * 0.05
        return {'inputs': inputs, 'filter_0': filter_0, 'filter_1': filter_1}
    _L0_rec_all = _L0_rec_setup()
    _L0_rec_in = {k: v for k, v in _L0_rec_all.items() if k in ('filter_0', 'filter_1')}
    del _L0_rec_all
    return {'dense_ctx': dense_ctx, 'ids': ids, 'tbl_0': tbl_0, 'tbl_1': tbl_1, 'tbl_2': tbl_2, 'tbl_3': tbl_3, 'tbl_4': tbl_4, 'tbl_5': tbl_5, 'tbl_6': tbl_6, 'tbl_7': tbl_7, 'tbl_8': tbl_8, 'tbl_9': tbl_9, 'tbl_10': tbl_10, 'tbl_11': tbl_11, 'tbl_12': tbl_12, 'tbl_13': tbl_13, 'tbl_14': tbl_14, 'tbl_15': tbl_15, 'tbl_16': tbl_16, 'tbl_17': tbl_17, 'tbl_18': tbl_18, 'tbl_19': tbl_19, 'tbl_20': tbl_20, 'tbl_21': tbl_21, 'tbl_22': tbl_22, 'tbl_23': tbl_23, 'tbl_24': tbl_24, 'tbl_25': tbl_25, 'tbl_26': tbl_26, 'tbl_27': tbl_27, 'tbl_28': tbl_28, 'tbl_29': tbl_29, 'tbl_30': tbl_30, 'tbl_31': tbl_31, 'W_top1': W_top1, 'b_top1': b_top1, 'W_top2': W_top2, 'b_top2': b_top2, 'W_top3': W_top3, 'L0_rec_filter_0': _L0_rec_in['filter_0'], 'L0_rec_filter_1': _L0_rec_in['filter_1']}

def reference(dense_ctx, ids, tbl_0, tbl_1, tbl_2, tbl_3, tbl_4, tbl_5, tbl_6, tbl_7, tbl_8, tbl_9, tbl_10, tbl_11, tbl_12, tbl_13, tbl_14, tbl_15, tbl_16, tbl_17, tbl_18, tbl_19, tbl_20, tbl_21, tbl_22, tbl_23, tbl_24, tbl_25, tbl_26, tbl_27, tbl_28, tbl_29, tbl_30, tbl_31, W_top1, b_top1, W_top2, b_top2, W_top3, L0_rec_filter_0, L0_rec_filter_1):
    import jax
    import jax.numpy as jnp

    def _L0_rec_ref(inputs, filter_0, filter_1):
        import jax, jax.numpy as jnp
        import numpy as np
        B, F, D = (512, 32, 32)
        LAYER_SIZE = [128, 128]

        def _cin_forward(inputs, filters):
            x0 = inputs
            prev = inputs
            outs = []
            for W in filters:
                z = jnp.einsum('bhd,bmd->bhmd', x0, prev)
                b, h, m, d = z.shape
                z = z.reshape(b, h * m, d)
                cur = jnp.einsum('bpd,pn->bnd', z, W[0])
                cur = jax.nn.relu(cur)
                prev = cur
                outs.append(cur)
            result = jnp.concatenate(outs, axis=1)
            return jnp.sum(result, axis=-1)
        return _cin_forward(inputs, (filter_0, filter_1))
    e = jnp.stack([tbl_0[ids[:, 0]], tbl_1[ids[:, 1]], tbl_2[ids[:, 2]], tbl_3[ids[:, 3]], tbl_4[ids[:, 4]], tbl_5[ids[:, 5]], tbl_6[ids[:, 6]], tbl_7[ids[:, 7]], tbl_8[ids[:, 8]], tbl_9[ids[:, 9]], tbl_10[ids[:, 10]], tbl_11[ids[:, 11]], tbl_12[ids[:, 12]], tbl_13[ids[:, 13]], tbl_14[ids[:, 14]], tbl_15[ids[:, 15]], tbl_16[ids[:, 16]], tbl_17[ids[:, 17]], tbl_18[ids[:, 18]], tbl_19[ids[:, 19]], tbl_20[ids[:, 20]], tbl_21[ids[:, 21]], tbl_22[ids[:, 22]], tbl_23[ids[:, 23]], tbl_24[ids[:, 24]], tbl_25[ids[:, 25]], tbl_26[ids[:, 26]], tbl_27[ids[:, 27]], tbl_28[ids[:, 28]], tbl_29[ids[:, 29]], tbl_30[ids[:, 30]], tbl_31[ids[:, 31]]], axis=1)
    z = _L0_rec_ref(e, L0_rec_filter_0, L0_rec_filter_1)
    z = z.reshape(z.shape[0], -1)
    h = jnp.concatenate([z, dense_ctx], axis=1)
    h = jnp.maximum(h @ W_top1 + b_top1, 0.0)
    h = jnp.maximum(h @ W_top2 + b_top2, 0.0)
    y = h @ W_top3
    return y

_drawn_inputs = setup_inputs


def setup_inputs(seed=0):
    import zlib

    import numpy as np

    out = dict(_drawn_inputs(seed))
    spreads = {'b_top1': (0.0, 0.428), 'b_top2': (0.0, 0.413)}
    factors = {'tbl_0': 5.817,
     'tbl_1': 6.015,
     'tbl_2': 5.99,
     'tbl_3': 6.175,
     'tbl_4': 6.009,
     'tbl_5': 5.873,
     'tbl_6': 6.41,
     'tbl_7': 6.392,
     'tbl_8': 6.096,
     'tbl_9': 5.859,
     'tbl_10': 5.902,
     'tbl_11': 6.216,
     'tbl_12': 5.805,
     'tbl_13': 5.879,
     'tbl_14': 5.703,
     'tbl_15': 6.048,
     'tbl_16': 5.959,
     'tbl_17': 5.85,
     'tbl_18': 6.006,
     'tbl_19': 6.063,
     'tbl_20': 5.933,
     'tbl_21': 6.457,
     'tbl_22': 5.795,
     'tbl_23': 6.009,
     'tbl_24': 6.114,
     'tbl_25': 5.715,
     'tbl_26': 6.091,
     'tbl_27': 6.184,
     'tbl_28': 5.927,
     'tbl_29': 6.397,
     'tbl_30': 6.218,
     'tbl_31': 5.701,
     'L0_rec_filter_1': 8.0}
    for name, (base, spread) in spreads.items():
        noise = np.random.default_rng([zlib.crc32(name.encode()), seed]).standard_normal(out[name].shape)
        drawn = base * np.exp(spread * noise) if base else spread * noise
        out[name] = jnp.asarray(drawn.astype(out[name].dtype))
    for name, factor in factors.items():
        out[name] = (out[name] * factor).astype(out[name].dtype)
    return out
```

```python
from contextlib import ExitStack

import concourse.bass as bass
from concourse import mybir

ALU = mybir.AluOpType
ACT = mybir.ActivationFunctionType
F32 = mybir.dt.float32
F32R = mybir.dt.float32r
I32 = mybir.dt.int32

P = 128
N_IN_FLIGHT = 4


def cin_tower(nc, dense_ctx, ids, tables, W_top1, b_top1, W_top2, b_top2, W_top3,
              filter_0, filter_1, eye, fold_scale, out):
    B, D_CTX = dense_ctx.shape
    F = ids.shape[1]
    D = tables[0].shape[1]
    N = filter_0.shape[2]
    H1 = W_top1.shape[1]
    H2 = W_top2.shape[1]
    BT = B // P
    DC = 4
    C = DC * P
    CPB = D // DC
    CHUNKS = BT * CPB
    ROWS = F + 16
    KT = 4
    J = N // 32
    G = F // 4
    GS = G // 2
    L1_PAIRS = J * GS // 2
    L0_PAIRS = KT // 2
    PAIRS = L1_PAIRS + L0_PAIRS
    R = N_IN_FLIGHT
    assert (F, D, N, B % P) == (32, 32, 128, 0)
    assert (2 * PAIRS) % R == 0 and (2 * L0_PAIRS) % R == 0 and L1_PAIRS % R == 0

    xt = nc.dram_tensor("xt_scratch", (CHUNKS, ROWS, C), F32).ap()
    w0_mm = nc.dram_tensor("w0_second_index_twice", (F, 2 * F, N), F32).ap()
    w0_hh = nc.dram_tensor("w0_first_index_twice", (2 * F, F, N), F32).ap()
    CH = ROWS * C

    with ExitStack() as ctx:
        def sb(name, shape, dt=F32):
            return ctx.enter_context(nc.sbuf_tensor(name, shape, dt))

        def psum(name, shape):
            return ctx.enter_context(nc.psum_tensor(name, shape, F32))

        def sem(name):
            return ctx.enter_context(nc.semaphore(name))

        acc0 = psum("acc0", [P, C])
        acc1 = psum("acc1", [P, C])
        prev_ps = psum("prev_ps", [P, 2, C])
        turn_ps = prev_ps[:, 1, :]
        prod = psum("prod", [P, 2, 2, C])

        identity = sb("identity", [P, P])
        halves = sb("halves", [P, 1])
        idx = sb("idx", [P, F], I32)
        emb = sb("emb", [P, F * D])
        emb_sorted = sb("emb_sorted", [P, CPB, F * DC])
        xt_stage = sb("xt_stage", [P, CPB, P])

        xa = sb("xa", [P, 2, G, C])
        xb = sb("xb", [P, KT, C])
        xm = sb("xm", [P, C])
        x16 = sb("x16", [16, 2, C])
        prev = sb("prev", [P, 2, C])
        prev_rep = sb("prev_rep", [P, 2, J, C])
        relu1 = sb("relu1", [P, 2, C])
        hi = sb("hi", [P, R, 2, C], F32R)
        lo = sb("lo", [P, R, 2, C], F32R)
        whole = sb("whole", [P, R, 2, C])
        small = sb("small", [16, C])
        small_hi = sb("small_hi", [16, C], F32R)
        small_lo = sb("small_lo", [16, C], F32R)

        w1_raw = sb("w1_raw", [P, J, GS, N])
        w1_hi = sb("w1_hi", [P, J, GS, N], F32R)
        w1_lo = sb("w1_lo", [P, J, GS, N], F32R)
        w1_whole = sb("w1_whole", [P, J, G - GS, N])
        w0_a = sb("w0_a", [P, KT, N])
        w0_b = sb("w0_b", [P, KT, N])
        w0_hi = sb("w0_hi", [P, KT, N], F32R)
        w0_lo = sb("w0_lo", [P, KT, N], F32R)
        w16_a = sb("w16_a", [16, N])
        w16_b = sb("w16_b", [16, N])
        w16_hi = sb("w16_hi", [16, N], F32R)
        w16_lo = sb("w16_lo", [16, N], F32R)

        sum0 = sb("sum0", [P, C])
        sum1 = sb("sum1", [P, C])
        half_sum = sb("half_sum", [P, 2, 2 * P])
        pooled0 = sb("pooled0", [P, BT, P])
        pooled1 = sb("pooled1", [P, BT + 1, P])
        ctx_in = sb("ctx_in", [P, BT, D_CTX])
        ctx_t = sb("ctx_t", [D_CTX, B])
        wt1_sb = sb("wt1_sb", [P, 2, H1])
        wt1_ctx = sb("wt1_ctx", [D_CTX, H1])
        wt2_sb = sb("wt2_sb", [P, H1 // P, H2])
        wt3_sb = sb("wt3_sb", [P, H2 // P])
        bt1_sb = sb("bt1_sb", [P, H1 // P])
        bt2_sb = sb("bt2_sb", [P, H2 // P])
        h1 = xa[:, 0, 0:H1 // P, :]
        h2 = xa[:, 1, 0:H2 // P, :]
        y = small[0:1, :]

        ids_loaded = sem("ids_loaded")
        consts_loaded = sem("consts_loaded")
        w0_doubled = sem("w0_doubled")
        w0_loaded = sem("w0_loaded")
        w1_loaded = sem("w1_loaded")
        tower_loaded = sem("tower_loaded")
        w0_folded = sem("w0_folded")
        w_hi_ready = sem("w_hi_ready")
        w_lo_ready = sem("w_lo_ready")
        gathered = sem("gathered")
        sorted_d = sem("sorted_d")
        transposed = sem("transposed")
        xt_staged = sem("xt_staged")
        xt_written = sem("xt_written")
        l0_loaded = sem("l0_loaded")
        xa_loaded = [sem(f"xa_loaded_{q}") for q in range(2)]
        prev_replicated = [sem(f"prev_replicated_{q}") for q in range(2)]
        prev_in_psum = sem("prev_in_psum")
        product_ready = sem("product_ready")
        hi_ready = sem("hi_ready")
        lo_ready = sem("lo_ready")
        split_used = sem("split_used")
        small_ready = sem("small_ready")
        small_hi_ready = sem("small_hi_ready")
        small_lo_ready = sem("small_lo_ready")
        whole_ready = sem("whole_ready")
        whole_free = sem("whole_free")
        l0_done = sem("l0_done")
        l0_evacuated = sem("l0_evacuated")
        l1_cleared = sem("l1_cleared")
        l1_evacuated = sem("l1_evacuated")
        summed0 = sem("summed0")
        summed1 = sem("summed1")
        folded0 = sem("folded0")
        folded1 = sem("folded1")
        ctx_turned = sem("ctx_turned")
        ctx_ready = sem("ctx_ready")
        tower_mm = sem("tower_mm")
        tower_relu = sem("tower_relu")
        y_ready = sem("y_ready")
        y_written = sem("y_written")

        def split_base(c):
            return 2 * L0_PAIRS + PAIRS * c

        LAST_BASE = split_base(CHUNKS - 2) + L1_PAIRS

        def loop_chunks(eng, body, prep, begin=None):
            with eng.Fori(0, BT - 1) as bt:
                if begin:
                    begin(bt + 1)
                with eng.Fori(0, CPB // 2 - 1) as pair:
                    body(bt * (CPB // 2) + pair)
                prep(bt + 1)
                body(bt * (CPB // 2) + (CPB // 2 - 1))
            with eng.Fori((BT - 1) * (CPB // 2), CHUNKS // 2 - 1) as half:
                body(half)

        def dram(tensor, offset, dims):
            return bass.AP(tensor.tensor, offset, dims)

        block = ctx.enter_context(nc.Block())

        @block.sync
        def _(sp):
            sp.dma_start(idx[:], ids[0:P, :]).then_inc(ids_loaded, 16)
            sp.dma_start(identity[:], eye).then_inc(consts_loaded, 16)
            sp.dma_start(halves[:], fold_scale).then_inc(consts_loaded, 16)
            sp.dma_start(ctx_in[:], dense_ctx.rearrange("(t p) f -> p t f", p=P)).then_inc(consts_loaded, 16)

            for j in range(J):
                for g in range(G):
                    dst = w1_raw[:, j, g, :] if g < GS else w1_whole[:, j, g - GS, :]
                    src = dram(filter_1, (g * N + 32 * j) * N, [[N, 32], [G * N * N, 4], [1, N]])
                    sp.dma_start(dst, src).then_inc(w1_loaded, 16)

            def work_out(x):
                return sp.snap(sp.to_reg(x))

            def load_ids(bt):
                at = bt * (P * F) if isinstance(bt, int) else work_out(bt * (P * F))
                sp.dma_start(idx[:], dram(ids, at, [[F, P], [1, F]])).then_inc(ids_loaded, 16)

            def write_xt(bt):
                value = int if isinstance(bt, int) else work_out
                first = bt * (CPB * CH)
                staged, written = value(2 * bt + 2), value(32 * bt + 32)
                sp.wait_ge(xt_staged, staged)
                sp.dma_start(dram(xt, first, [[P, P], [CH, CPB], [1, P]]), xt_stage[:]).then_inc(xt_written, 16)
                sp.dma_start(dram(xt, first + F * C, [[P, 64], [CH, CPB], [1, P]]),
                             xt_stage[0:64]).then_inc(xt_written, 16)
                sp.wait_ge(xt_written, written)

            def load_l0(at):
                sp.dma_start(xb[:], dram(xt, at, [[C, F], [KT * C, 4], [1, KT * C]])).then_inc(l0_loaded, 16)
                sp.dma_start(xm[:], dram(xt, at, [[C, F], [0, 4], [1, C]])).then_inc(l0_loaded, 16)
                sp.dma_start(x16[:], dram(xt, at, [[C, 16], [16 * C, 2], [1, C]])).then_inc(l0_loaded, 16)

            def load_xa(at, q):
                sp.dma_start(xa[:, q], dram(xt, at, [[0, 32], [G * C, 4], [1, G * C]])).then_inc(
                    xa_loaded[q], 16)

            def replicate_prev(q):
                for j in range(J):
                    part = prev[32 * j:32 * (j + 1), q, :]
                    src = bass.AP(part.tensor, part.offset, [list(part.ap[0]), [0, 4], [1, C]])
                    sp.dma_start(prev_rep[:, q, j, :], src).then_inc(prev_replicated[q], 16)

            write_xt(0)
            load_l0(0)
            load_xa(0, 0)
            sp.wait_ge(small_ready, 1)
            load_l0(CH)
            load_xa(CH, 1)
            sp.wait_ge(l0_evacuated, 1)
            replicate_prev(0)

            def two_chunks(it, last=False):
                value = int if last else work_out
                for par in range(2):
                    c = 2 * it + par
                    next_but_one = (c + 2) * CH
                    c_plus_2, prev_copies = value(c + 2), value(J * c + 1)
                    wholes, wholes_after = value(L1_PAIRS * c + 1), value(L1_PAIRS * (c + 1))
                    products_after = value(split_base(c) + L1_PAIRS)
                    if not last:
                        sp.wait_ge(small_ready, c_plus_2)
                        load_l0(next_but_one)
                    if not (last and par):
                        sp.wait_ge(l0_evacuated, c_plus_2)
                        sp.wait_ge(prev_in_psum, prev_copies)
                        sp.wait_ge(whole_ready, wholes)
                        replicate_prev(1 - par)
                    if not last:
                        sp.wait_ge(product_ready, products_after)
                        sp.wait_ge(whole_ready, wholes_after)
                        load_xa(next_but_one, par)

            loop_chunks(sp, two_chunks, write_xt, load_ids)
            two_chunks(CHUNKS // 2 - 1, last=True)

            sp.wait_ge(y_ready, 1)
            sp.dma_start(out.rearrange("b o -> o b"), y).then_inc(y_written, 16)
            sp.wait_ge(y_written, 16)

        @block.gpsimd
        def _(pool):
            def gather(fields):
                for f in fields:
                    pool.indirect_dma_start(
                        emb[:, D * f:D * (f + 1)], None, tables[f],
                        bass.IndirectOffsetOnAxis(ap=idx[:, f:f + 1], axis=0)).then_inc(gathered, 16)

            pool.wait_ge(ids_loaded, 16)
            gather(range(F))
            pool.memset(sum0[:], 0.0).then_inc(summed0, 1)
            pool.memset(half_sum[:, 0, :], 0.0).then_inc(folded0, 1)
            pool.memset(sum1[:], 0.0).then_inc(summed1, 2)

            def fold(which, total, summed, count, folded, before, dst):
                pool.wait_ge(summed, count)
                pool.tensor_tensor(half_sum[:, which, :], total[:, 0:2 * P], total[:, 2 * P:C],
                                   ALU.add).then_inc(folded, 1)
                pool.wait_ge(folded, before + 1)
                pool.tensor_tensor(dst, half_sum[:, which, 0:P], half_sum[:, which, P:2 * P],
                                   ALU.add).then_inc(folded, 1)

            def chunk(bt, dg, gathers):
                c = bt * CPB + dg
                par = dg % 2
                for k in range(L1_PAIRS):
                    j, g = k // (GS // 2), GS + 2 * (k % (GS // 2))
                    if k == 0:
                        pool.wait_ge(xa_loaded[par], 16 * (bt * (CPB // 2) + dg // 2 + 1))
                        pool.wait_ge(prev_replicated[par], 16 * J * (bt * (CPB // 2) + dg // 2 + 1))
                    pool.wait_ge(whole_free, L1_PAIRS * c + k + 1)
                    pool.tensor_tensor(
                        whole[:, k % R], xa[:, par, g:g + 2, :],
                        prev_rep[:, par, j, None, :].to_broadcast([P, 2, C]), ALU.mult).then_inc(whole_ready, 1)
                    if gathers:
                        gather(gathers[k * len(gathers) // L1_PAIRS:(k + 1) * len(gathers) // L1_PAIRS])
                    if k == 2 and dg != 1:
                        pool.wait_ge(l1_evacuated, c + 1)
                        if dg == 2:
                            pool.wait_ge(folded1, 2 * bt + 2)
                            pool.tensor_tensor(sum1[:], relu1[:, 0, :], relu1[:, 1, :], ALU.add).then_inc(summed1, 2)
                        else:
                            pool.wait_ge(summed1, c + 2)
                            pool.tensor_tensor(sum1[:], sum1[:], relu1[:, par, :], ALU.add).then_inc(summed1, 1)
                        if dg == 0:
                            fold(1, sum1, summed1, c + 3, folded1, 2 * bt, pooled1[:, bt, :])
                    if k == 5 and dg != CPB - 1:
                        pool.wait_ge(l0_evacuated, c + 2)
                        if dg == 0:
                            pool.wait_ge(folded0, 2 * bt + 1)
                            pool.tensor_tensor(sum0[:], prev[:, 0, :], prev[:, 1, :], ALU.add).then_inc(summed0, 2)
                        else:
                            pool.wait_ge(summed0, c + 2)
                            pool.tensor_tensor(sum0[:], sum0[:], prev[:, 1 - par, :], ALU.add).then_inc(summed0, 1)
                        if dg == CPB - 2:
                            fold(0, sum0, summed0, c + 3, folded0, 2 * bt + 1, pooled0[:, bt, :])

            with pool.Fori(0, BT - 1) as bt:
                pool.wait_ge(ids_loaded, 16 * (bt + 2))
                pool.wait_ge(sorted_d, bt + 1)
                for dg in range(CPB):
                    chunk(bt, dg, range(F * dg // (CPB - 2), F * (dg + 1) // (CPB - 2)) if dg < CPB - 2 else None)
            for dg in range(CPB):
                chunk(BT - 1, dg, None)

            pool.wait_ge(l1_evacuated, CHUNKS + 1)
            pool.wait_ge(summed1, CHUNKS + 2)
            pool.tensor_tensor(sum1[:], sum1[:], relu1[:, 0, :], ALU.add).then_inc(summed1, 1)
            fold(1, sum1, summed1, CHUNKS + 3, folded1, 2 * BT, pooled1[:, BT, :])

        @block.scalar
        def _(act):
            for r in range(2):
                act.dma_start(dram(w0_mm, r * F * N, [[2 * F * N, F], [1, F * N]]),
                              dram(filter_0, 0, [[F * N, F], [1, F * N]])).then_inc(w0_doubled, 16)
                act.dma_start(dram(w0_hh, r * F * F * N, [[F * N, F], [1, F * N]]),
                              dram(filter_0, 0, [[F * N, F], [1, F * N]])).then_inc(w0_doubled, 16)
            act.dma_start(w16_a[:], dram(filter_0, 16 * N, [[(F + 1) * N, 16], [1, N]])).then_inc(w0_loaded, 16)
            act.dma_start(w16_b[:], dram(filter_0, 16 * F * N, [[(F + 1) * N, 16], [1, N]])).then_inc(w0_loaded, 16)
            act.wait_ge(w0_doubled, 64)
            act.dma_start(w0_a[:], dram(w0_mm, 0, [[(2 * F + 1) * N, F], [KT * N, 4], [1, KT * N]])).then_inc(
                w0_loaded, 16)
            for t in range(KT):
                act.dma_start(w0_b[:, t, :], dram(w0_hh, t * F * N, [[(F + 1) * N, F], [KT * F * N, 4], [1, N]])
                              ).then_inc(w0_loaded, 16)
            act.dma_start(wt1_sb[:], W_top1[0:2 * P, :].rearrange("(t p) n -> p t n", p=P)).then_inc(tower_loaded, 16)
            act.dma_start(wt1_ctx[:], W_top1[2 * N:2 * N + D_CTX, :]).then_inc(tower_loaded, 16)
            act.dma_start(wt2_sb[:], W_top2.rearrange("(t p) n -> p t n", p=P)).then_inc(tower_loaded, 16)
            with nc.allow_non_contiguous_dma(reason="a few hundred words, once"):
                act.dma_start(wt3_sb[:], W_top3.rearrange("(t p) n -> p (t n)", p=P)).then_inc(tower_loaded, 16)
                act.dma_start(bt1_sb[:], b_top1.rearrange("(t p) -> p t", p=P)).then_inc(tower_loaded, 16)
                act.dma_start(bt2_sb[:], b_top2.rearrange("(t p) -> p t", p=P)).then_inc(tower_loaded, 16)

            act.wait_ge(w0_folded, 3)
            act.activation(w0_hi[:], w0_a[:], ACT.Copy).then_inc(w_hi_ready, 1)
            act.activation(w16_hi[:], w16_a[:], ACT.Copy).then_inc(w_hi_ready, 1)
            act.wait_ge(w1_loaded, 16 * J * G)
            act.activation(w1_hi[:], w1_raw[:], ACT.Copy).then_inc(w_hi_ready, 1)

            act.wait_ge(ctx_turned, 1)
            act.activation(ctx_t[:], acc0[0:D_CTX, :], ACT.Copy).then_inc(ctx_ready, 1)

            def stage_xt(bt):
                act.wait_ge(gathered, 16 * F * (bt + 1))
                if not isinstance(bt, int):
                    act.wait_ge(transposed, 2 * bt)
                act.activation(emb_sorted[:].rearrange("b g (h d) -> b g h d", h=F),
                               emb[:].rearrange("b (h g d) -> b g h d", h=F, g=CPB),
                               ACT.Copy).then_inc(sorted_d, 1)
                for half in range(2):
                    act.wait_ge(transposed, 2 * bt + half + 1)
                    if half == 0 and not isinstance(bt, int):
                        act.wait_ge(xt_written, 32 * bt)
                    act.activation(xt_stage[:, 4 * half:4 * half + 4, :], turn_ps, ACT.Copy).then_inc(xt_staged, 1)
                act.wait_ge(xt_staged, 2 * bt + 2)

            def split_high(n, slot):
                act.wait_ge(product_ready, n + 1)
                act.activation(hi[:, slot % R], prod[:, slot % 2], ACT.Copy).then_inc(hi_ready, 1)

            def small_high(c):
                act.wait_ge(small_ready, c + 1)
                act.activation(small_hi[:], small[:], ACT.Copy).then_inc(small_hi_ready, 1)

            def relu_l0(c, q):
                act.wait_ge(l0_done, c + 1)
                act.activation(prev[:, q, :], acc0[:], ACT.Relu).then_inc(l0_evacuated, 1)

            stage_xt(0)
            for c in range(2):
                if c == 1:
                    act.wait_ge(small_lo_ready, 1)
                    act.wait_ge(l0_done, 1)
                for k in range(L0_PAIRS):
                    split_high(L0_PAIRS * c + k, L0_PAIRS * c + k)
                small_high(c)
                if c == 0:
                    relu_l0(0, 0)
            act.wait_ge(prev_replicated[0], 16 * J)
            act.activation(prev_ps[:, 0, :], prev_rep[:, 0, 0, :], ACT.Copy).then_inc(prev_in_psum, 1)

            def chunk(it, par, base, last):
                c = 2 * it + par
                b0 = PAIRS * par if not last else (PAIRS * 0 if par == 0 else L1_PAIRS)
                for k in range(L1_PAIRS):
                    if k % 2 == 0:
                        j = k // 2 + 1
                        if j < J:
                            act.wait_ge(product_ready, base + k if k else base - L0_PAIRS)
                            act.activation(prev_ps[:, j % 2, :], prev_rep[:, par, j, :], ACT.Copy).then_inc(
                                prev_in_psum, 1)
                        elif not (last and par):
                            act.wait_ge(product_ready, base + k)
                            act.wait_ge(prev_replicated[1 - par], 16 * J * (it + 1 + par))
                            act.activation(prev_ps[:, 0, :], prev_rep[:, 1 - par, 0, :], ACT.Copy).then_inc(
                                prev_in_psum, 1)
                    act.wait_ge(split_used, base + k - R + 1)
                    split_high(base + k, b0 + k)
                    if k == 1:
                        act.wait_ge(l1_cleared, 1)
                        act.wait_ge(whole_free, L1_PAIRS * c + R)
                        act.wait_ge(summed1, c + 1)
                        act.activation(relu1[:, par, :], acc1[:], ACT.Relu).then_inc(l1_evacuated, 1)
                    if k == 3 and not (last and par):
                        act.wait_ge(summed0, c + 1)
                        relu_l0(c + 1, 1 - par)
                if not last:
                    for k in range(L1_PAIRS, PAIRS):
                        act.wait_ge(split_used, base + k - R + 1)
                        split_high(base + k, b0 + k)
                    act.wait_ge(l0_done, c + 2)
                    small_high(c + 2)

            def two_chunks(it):
                for par in range(2):
                    chunk(it, par, split_base(2 * it + par), False)

            loop_chunks(act, two_chunks, stage_xt)
            chunk(CHUNKS // 2 - 1, 0, split_base(CHUNKS - 2), True)
            chunk(CHUNKS // 2 - 1, 1, LAST_BASE, True)
            act.wait_ge(whole_free, L1_PAIRS * CHUNKS + R)
            act.wait_ge(summed1, CHUNKS + 1)
            act.activation(relu1[:, 0, :], acc1[:], ACT.Relu).then_inc(l1_evacuated, 1)

            act.wait_ge(tower_loaded, 16 * 6)
            for q in range(H1 // P):
                act.wait_ge(tower_mm, q + 1)
                act.activation(h1[:, q, :], prod[:, q // 2, q % 2, :], ACT.Relu,
                               bias=bt1_sb[:, q:q + 1]).then_inc(tower_relu, 1)
            for q in range(H2 // P):
                act.wait_ge(tower_mm, H1 // P + q + 1)
                act.activation(h2[:, q, :], prev_ps[:, q, :], ACT.Relu,
                               bias=bt2_sb[:, q:q + 1]).then_inc(tower_relu, 1)
            act.wait_ge(tower_mm, H1 // P + H2 // P + 1)
            act.activation(y, acc0[0:1, :], ACT.Copy).then_inc(y_ready, 1)

        @block.vector
        def _(dve):
            dve.memset(acc1[:], 0.0).then_inc(l1_cleared, 1)
            dve.wait_ge(consts_loaded, 48)
            dve.wait_ge(w0_loaded, 16 * (3 + KT))
            dve.tensor_tensor(w0_a[:], w0_a[:], w0_b[:], ALU.add).then_inc(w0_folded, 1)
            dve.tensor_tensor(w16_a[:], w16_a[:], w16_b[:], ALU.add).then_inc(w0_folded, 1)
            dve.wait_ge(w0_folded, 2)
            dve.tensor_scalar(w0_a[:, 0, :], w0_a[:, 0, :], halves[:, 0:1], None, ALU.mult).then_inc(w0_folded, 1)
            dve.wait_ge(w0_folded, 3)
            dve.wait_ge(w_hi_ready, 2)
            dve.tensor_tensor(w0_lo[:], w0_a[:], w0_hi[:].bitcast(F32), ALU.subtract).then_inc(w_lo_ready, 1)
            dve.tensor_tensor(w16_lo[:], w16_a[:], w16_hi[:].bitcast(F32), ALU.subtract).then_inc(w_lo_ready, 1)
            dve.wait_ge(w_hi_ready, 3)
            dve.tensor_tensor(w1_lo[:], w1_raw[:], w1_hi[:].bitcast(F32), ALU.subtract).then_inc(w_lo_ready, 1)

            def low(n, slot):
                dve.wait_ge(hi_ready, n + 1)
                dve.tensor_tensor(lo[:, slot % R], prod[:, slot % 2], hi[:, slot % R].bitcast(F32),
                                  ALU.subtract).then_inc(lo_ready, 1)

            def product_l0(t, slot):
                dve.tensor_tensor(prod[:, slot % 2], xb[:, 2 * t:2 * t + 2, :],
                                  xm[:, None, :].to_broadcast([P, 2, C]), ALU.mult).then_inc(product_ready, 1)

            def small_product():
                dve.tensor_tensor(small[:], x16[:, 0, :], x16[:, 1, :], ALU.mult).then_inc(small_ready, 1)

            def small_low(c):
                dve.wait_ge(small_hi_ready, c + 1)
                dve.tensor_tensor(small_lo[:], small[:], small_hi[:].bitcast(F32),
                                  ALU.subtract).then_inc(small_lo_ready, 1)

            for c in range(2):
                n = L0_PAIRS * c
                dve.wait_ge(l0_loaded, 48 * (c + 1))
                if c:
                    dve.wait_ge(lo_ready, n)
                    dve.wait_ge(small_lo_ready, 1)
                product_l0(0, n)
                product_l0(1, n + 1)
                if c:
                    dve.wait_ge(l0_done, 1)
                small_product()
                low(n, n)
                low(n + 1, n + 1)
                small_low(c)

            def chunk(it, par, base, last):
                c = 2 * it + par
                b0 = PAIRS * par if not last else (PAIRS * 0 if par == 0 else L1_PAIRS)
                pairs = L1_PAIRS if last else PAIRS
                dve.wait_ge(xa_loaded[par], 16 * (it + 1))
                for k in range(pairs):
                    dve.wait_ge(lo_ready, base + k - 1)
                    if k < L1_PAIRS:
                        j, g = k // 2, 2 * (k % 2)
                        if k % 2 == 0:
                            dve.wait_ge(prev_in_psum, J * c + j + 1)
                        dve.tensor_tensor(prod[:, (b0 + k) % 2], xa[:, par, g:g + 2, :],
                                          prev_ps[:, j % 2, None, :].to_broadcast([P, 2, C]),
                                          ALU.mult).then_inc(product_ready, 1)
                    else:
                        if k == L1_PAIRS:
                            dve.wait_ge(l0_loaded, 48 * (c + 3))
                        product_l0(k - L1_PAIRS, b0 + k)
                    if k:
                        dve.wait_ge(split_used, base + k - R)
                        low(base + k - 1, b0 + k - 1)
                if not last:
                    dve.wait_ge(small_lo_ready, c + 2)
                    small_product()
                dve.wait_ge(split_used, base + pairs - R)
                low(base + pairs - 1, b0 + pairs - 1)
                if not last:
                    dve.wait_ge(l0_done, c + 2)
                    small_low(c + 2)

            with dve.Fori(0, CHUNKS // 2 - 1) as it:
                for par in range(2):
                    chunk(it, par, split_base(2 * it + par), False)
            chunk(CHUNKS // 2 - 1, 0, split_base(CHUNKS - 2), True)
            chunk(CHUNKS // 2 - 1, 1, LAST_BASE, True)

        @block.tensor
        def _(pe):
            pe.sem_inc(whole_free, R)
            pe.wait_ge(consts_loaded, 48)
            for t in range(BT):
                turn = pe.transpose(acc0[0:D_CTX, P * t:P * (t + 1)], ctx_in[:, t, :], identity[:])
            turn.then_inc(ctx_turned, 1)
            pe.wait_ge(ctx_ready, 1)

            def transpose_x(bt):
                pe.wait_ge(sorted_d, bt + 1)
                for half in range(2):
                    if half == 1:
                        pe.wait_ge(xt_staged, 2 * bt + 1)
                    for q in range(4):
                        turn = pe.transpose(turn_ps[:, P * q:P * (q + 1)], emb_sorted[:, 4 * half + q, :], identity[:])
                    turn.then_inc(transposed, 1)

            def three_passes(acc, w_hi, w_lo, v_hi, v_lo, start, stop):
                pe.matmul(acc, w_hi, v_hi, start=start, stop=False)
                pe.matmul(acc, w_hi, v_lo, start=False, stop=False)
                return pe.matmul(acc, w_lo, v_hi, start=False, stop=stop)

            def layer0(c, n, slot):
                for t in range(KT):
                    if t % 2 == 0:
                        pe.wait_ge(lo_ready, n + t // 2 + 1)
                    s = (slot + t // 2) % R
                    mm = three_passes(acc0[:], w0_hi[:, t, :], w0_lo[:, t, :], hi[:, s, t % 2, :],
                                      lo[:, s, t % 2, :], t == 0, False)
                    if t % 2 == 1:
                        mm.then_inc(split_used, 1)
                pe.wait_ge(small_lo_ready, c + 1)
                three_passes(acc0[:], w16_hi[:], w16_lo[:], small_hi[:], small_lo[:], False, True).then_inc(
                    l0_done, 1)

            transpose_x(0)
            pe.wait_ge(w_lo_ready, 3)
            layer0(0, 0, 0)
            pe.wait_ge(l0_evacuated, 1)
            layer0(1, L0_PAIRS, L0_PAIRS)

            def chunk(it, par, base, last):
                c = 2 * it + par
                b0 = PAIRS * par if not last else (PAIRS * 0 if par == 0 else L1_PAIRS)
                pe.wait_ge(l1_evacuated, c + 1)
                for k in range(L1_PAIRS):
                    j, g = k // 2, 2 * (k % 2)
                    s = (b0 + k) % R
                    pe.wait_ge(lo_ready, base + k + 1)
                    for u in range(2):
                        mm = three_passes(acc1[:], w1_hi[:, j, g + u, :], w1_lo[:, j, g + u, :],
                                          hi[:, s, u, :], lo[:, s, u, :], k == 0 and u == 0, False)
                    mm.then_inc(split_used, 1)
                    pe.wait_ge(whole_ready, L1_PAIRS * c + k + 1)
                    for u in range(2):
                        mm = pe.matmul(acc1[:], w1_whole[:, j, g + u, :], whole[:, k % R, u, :],
                                       start=False, stop=k == L1_PAIRS - 1 and u == 1)
                    mm.then_inc(whole_free, 1)
                if not last:
                    pe.wait_ge(l0_evacuated, c + 2)
                    layer0(c + 2, base + L1_PAIRS, b0 + L1_PAIRS)

            def two_chunks(it):
                for par in range(2):
                    chunk(it, par, split_base(2 * it + par), False)

            def prep(bt):
                pe.wait_ge(product_ready, split_base(bt * CPB) + (L1_PAIRS - 3 * PAIRS))
                transpose_x(bt)

            loop_chunks(pe, two_chunks, prep)
            chunk(CHUNKS // 2 - 1, 0, split_base(CHUNKS - 2), True)
            chunk(CHUNKS // 2 - 1, 1, LAST_BASE, True)

            pe.wait_ge(tower_loaded, 16 * 6)
            pe.wait_ge(folded1, 2 * BT + 2)
            for q in range(H1 // P):
                cols = slice(P * q, P * (q + 1))
                a = prod[:, q // 2, q % 2, :]
                pe.matmul(a, wt1_sb[:, 0, cols], pooled0[:], start=True, stop=False)
                pe.matmul(a, wt1_ctx[:, cols], ctx_t[:], start=False, stop=False)
                pe.matmul(a, wt1_sb[:, 1, cols], pooled1[:, 1:BT + 1, :], start=False, stop=True).then_inc(tower_mm, 1)
            for q in range(H2 // P):
                for t in range(H1 // P):
                    pe.wait_ge(tower_relu, t + 1)
                    mm = pe.matmul(prev_ps[:, q, :], wt2_sb[:, t, P * q:P * (q + 1)], h1[:, t, :],
                                   start=t == 0, stop=t == H1 // P - 1)
                mm.then_inc(tower_mm, 1)
            for t in range(H2 // P):
                pe.wait_ge(tower_relu, H1 // P + t + 1)
                mm = pe.matmul(acc0[0:1, :], wt3_sb[:, t:t + 1], h2[:, t, :], start=t == 0, stop=t == H2 // P - 1)
            mm.then_inc(tower_mm, 1)


def kernel(**inputs):
    import numpy as np
    import concourse.bacc as bacc
    from concourse.bass_utils import run_bass_kernel_spmd

    nc = bacc.Bacc("TRN2", target_bir_lowering=False, num_devices=1)
    arrays = {}

    def given(name, a):
        arrays[f"in_{name}"] = np.ascontiguousarray(a)
        a = arrays[f"in_{name}"]
        return nc.dram_tensor(f"in_{name}", a.shape, mybir.dt.from_np(a.dtype), kind="ExternalInput").ap()

    n_fields = inputs["ids"].shape[1]
    scale = np.ones((P, 1), np.float32)
    scale[::4] = 0.5
    args = [given("dense_ctx", inputs["dense_ctx"]), given("ids", inputs["ids"]),
            [given(f"tbl_{f}", inputs[f"tbl_{f}"]) for f in range(n_fields)]]
    args += [given(n, inputs[n]) for n in ("W_top1", "b_top1", "W_top2", "b_top2", "W_top3",
                                           "L0_rec_filter_0", "L0_rec_filter_1")]
    args += [given("eye", np.eye(P, dtype=np.float32)), given("fold_scale", scale)]
    y = nc.dram_tensor("y", (inputs["ids"].shape[0], 1), F32, kind="ExternalOutput").ap()
    cin_tower(nc, *args, y)
    r = run_bass_kernel_spmd(nc, [arrays], core_ids=[0])
    return r.results[0]["y"]
```

```python
from contextlib import ExitStack

import concourse.bass as bass
from concourse import mybir

ALU = mybir.AluOpType
ACT = mybir.ActivationFunctionType
F32 = mybir.dt.float32
F32R = mybir.dt.float32r
I32 = mybir.dt.int32

P = 128
N_IN_FLIGHT = 4


def cin_tower(nc, dense_ctx, ids, tables, W_top1, b_top1, W_top2, b_top2, W_top3,
              filter_0, filter_1, eye, fold_scale, out):
    B, D_CTX = dense_ctx.shape
    F = ids.shape[1]
    D = tables[0].shape[1]
    N = filter_0.shape[2]
    H1 = W_top1.shape[1]
    H2 = W_top2.shape[1]
    BT = B // P
    DC = 4
    C = DC * P
    CPB = D // DC
    CHUNKS = BT * CPB
    ROWS = F + 16
    KT = 4
    J = N // 32
    G = F // 4
    GS = G // 2
    L1_PAIRS = J * GS // 2
    L0_PAIRS = KT // 2
    PAIRS = L1_PAIRS + L0_PAIRS
    EARLY = 3 * F // 4
    R = N_IN_FLIGHT
    assert (F, D, N, B % P) == (32, 32, 128, 0)
    assert (2 * PAIRS) % R == 0 and (2 * L0_PAIRS) % R == 0 and L1_PAIRS % R == 0

    xt = nc.dram_tensor("xt_scratch", (CHUNKS, ROWS, C), F32).ap()
    w0_mm = nc.dram_tensor("w0_second_index_twice", (F, 2 * F, N), F32).ap()
    w0_hh = nc.dram_tensor("w0_first_index_twice", (2 * F, F, N), F32).ap()
    CH = ROWS * C

    with ExitStack() as ctx:
        def sb(name, shape, dt=F32):
            return ctx.enter_context(nc.sbuf_tensor(name, shape, dt))

        def psum(name, shape):
            return ctx.enter_context(nc.psum_tensor(name, shape, F32))

        def sem(name):
            return ctx.enter_context(nc.semaphore(name))

        acc0 = psum("acc0", [P, C])
        acc1 = psum("acc1", [P, C])
        prev_ps = psum("prev_ps", [P, 2, C])
        prod = psum("prod", [P, 2, 2, C])

        identity = sb("identity", [P, P])
        halves = sb("halves", [P, 1])
        idx = sb("idx", [P, F], I32)
        emb = sb("emb", [P, F * D])
        emb_sorted = sb("emb_sorted", [P, CPB, F * DC])
        xt_stage = sb("xt_stage", [P, CPB, P])

        xa = sb("xa", [P, 2, G, C])
        xb = sb("xb", [P, KT, C])
        xm = sb("xm", [P, C])
        x16 = sb("x16", [3 * F, 2, C])
        prev = sb("prev", [P, 2, C])
        prev_rep = sb("prev_rep", [P, 2, J, C])
        relu1 = sb("relu1", [P, 2, C])
        hi = sb("hi", [P, R, 2, C], F32R)
        lo = sb("lo", [P, R, 2, C], F32R)
        whole = sb("whole", [P, R, 2, C])
        small = sb("small", [3 * F, C])
        small_split = sb("small_split", [3 * F, C], F32R)

        w1_raw = sb("w1_raw", [P, J, GS, N])
        w1_hi = sb("w1_hi", [P, J, GS, N], F32R)
        w1_lo = sb("w1_lo", [P, J, GS, N], F32R)
        w1_whole = sb("w1_whole", [P, J, G - GS, N])
        w0_a = sb("w0_a", [P, KT, N])
        w0_b = sb("w0_b", [P, KT, N])
        w0_hi = sb("w0_hi", [P, KT, N], F32R)
        w0_lo = sb("w0_lo", [P, KT, N], F32R)
        w16 = sb("w16", [3 * F, N])
        w16_split = sb("w16_split", [3 * F, N], F32R)

        sum0 = sb("sum0", [P, C])
        sum1 = sb("sum1", [P, C])
        half_sum = sb("half_sum", [P, 2, 2 * P])
        pooled0 = sb("pooled0", [P, BT, P])
        pooled1 = sb("pooled1", [P, BT + 1, P])
        ctx_in = sb("ctx_in", [P, BT, D_CTX])
        ctx_t = sb("ctx_t", [D_CTX, B])
        wt1_sb = sb("wt1_sb", [P, 2, H1])
        wt1_ctx = sb("wt1_ctx", [D_CTX, H1])
        wt2_sb = sb("wt2_sb", [P, H1 // P, H2])
        wt3_sb = sb("wt3_sb", [P, H2 // P])
        bt1_sb = sb("bt1_sb", [P, H1 // P])
        bt2_sb = sb("bt2_sb", [P, H2 // P])
        h1 = xa[:, 0, 0:H1 // P, :]
        h2 = xa[:, 1, 0:H2 // P, :]
        y = small[0:1, :]
        first_xb = prev_rep[:, 1]
        first_xm = relu1[:, 1, :]
        first_x16 = whole[0:3 * F, R - 1]

        ids_loaded = sem("ids_loaded")
        consts_loaded = sem("consts_loaded")
        w0_doubled = sem("w0_doubled")
        w0_loaded = sem("w0_loaded")
        w1_loaded = sem("w1_loaded")
        tower_loaded = sem("tower_loaded")
        w0_folded = sem("w0_folded")
        w_hi_ready = sem("w_hi_ready")
        w_lo_ready = sem("w_lo_ready")
        gathered_first = sem("gathered_first")
        gathered = sem("gathered")
        sorted_d = sem("sorted_d")
        transposed = sem("transposed")
        xt_staged = sem("xt_staged")
        xt_written = sem("xt_written")
        l0_loaded = sem("l0_loaded")
        l0_chunk_1_loaded = sem("l0_chunk_1_loaded")
        xa_loaded = [sem(f"xa_loaded_{q}") for q in range(2)]
        prev_replicated = [sem(f"prev_replicated_{q}") for q in range(2)]
        prev_in_psum = sem("prev_in_psum")
        product_ready = sem("product_ready")
        hi_ready = sem("hi_ready")
        lo_ready = sem("lo_ready")
        split_used = sem("split_used")
        small_ready = sem("small_ready")
        small_hi_ready = sem("small_hi_ready")
        small_lo_ready = sem("small_lo_ready")
        whole_ready = sem("whole_ready")
        whole_free = sem("whole_free")
        l0_done = sem("l0_done")
        l0_evacuated = sem("l0_evacuated")
        l1_cleared = sem("l1_cleared")
        l1_evacuated = sem("l1_evacuated")
        summed0 = sem("summed0")
        summed1 = sem("summed1")
        folded0 = sem("folded0")
        folded1 = sem("folded1")
        ctx_turned = sem("ctx_turned")
        ctx_ready = sem("ctx_ready")
        tower_mm = sem("tower_mm")
        tower_relu = sem("tower_relu")
        y_ready = sem("y_ready")
        y_written = sem("y_written")

        def split_base(c):
            return 2 * L0_PAIRS + PAIRS * c

        LAST_BASE = split_base(CHUNKS - 2) + L1_PAIRS

        def loop_chunks(eng, body, begin=None):
            with eng.Fori(0, BT - 1) as bt:
                if begin:
                    begin(bt + 1)
                with eng.Fori(0, CPB // 2 - 2) as pair:
                    body(bt * (CPB // 2) + pair)
                body(bt * (CPB // 2) + (CPB // 2 - 2), bt + 1)
                body(bt * (CPB // 2) + (CPB // 2 - 1))
            with eng.Fori((BT - 1) * (CPB // 2), CHUNKS // 2 - 1) as half:
                body(half)

        def dram(tensor, offset, dims):
            return bass.AP(tensor.tensor, offset, dims)

        block = ctx.enter_context(nc.Block())

        @block.sync
        def _(sp):
            sp.dma_start(idx[:], ids[0:P, :]).then_inc(ids_loaded, 16)
            sp.dma_start(identity[:], eye).then_inc(consts_loaded, 16)
            sp.dma_start(halves[:], fold_scale).then_inc(consts_loaded, 16)
            sp.dma_start(ctx_in[:], dense_ctx.rearrange("(t p) f -> p t f", p=P)).then_inc(consts_loaded, 16)

            for j in range(J):
                for g in range(G):
                    dst = w1_raw[:, j, g, :] if g < GS else w1_whole[:, j, g - GS, :]
                    src = dram(filter_1, (g * N + 32 * j) * N, [[N, 32], [G * N * N, 4], [1, N]])
                    sp.dma_start(dst, src).then_inc(w1_loaded, 16)

            def work_out(x):
                return sp.snap(sp.to_reg(x))

            def load_ids(bt):
                at = bt * (P * F) if isinstance(bt, int) else work_out(bt * (P * F))
                sp.dma_start(idx[:], dram(ids, at, [[F, P], [1, F]])).then_inc(ids_loaded, 16)

            def write_xt(first, half):
                at = first + half * (CPB // 2 * CH)
                part = xt_stage[:, CPB // 2 * half:CPB // 2 * (half + 1), :]
                sp.dma_start(dram(xt, at, [[P, P], [CH, CPB // 2], [1, P]]), part).then_inc(xt_written, 16)
                sp.dma_start(dram(xt, at + F * C, [[P, 64], [CH, CPB // 2], [1, P]]), part[0:64]).then_inc(xt_written, 16)

            def load_l0(at, x_b=xb[:], x_m=xm[:], x_16=x16[:], done=l0_loaded):
                sp.dma_start(x_b, dram(xt, at, [[C, F], [KT * C, 4], [1, KT * C]])).then_inc(done, 16)
                sp.dma_start(x_m, dram(xt, at, [[C, F], [0, 4], [1, C]])).then_inc(done, 16)
                for s in range(2):
                    sp.dma_start(x_16[:, s, :], dram(xt, at + 16 * C * s, [[0, 3], [C, F], [1, C]])).then_inc(
                        done, 16)

            def load_xa(at, q):
                sp.dma_start(xa[:, q], dram(xt, at, [[0, 32], [G * C, 4], [1, G * C]])).then_inc(
                    xa_loaded[q], 16)

            def replicate_prev(q):
                for j in range(J):
                    part = prev[32 * j:32 * (j + 1), q, :]
                    src = bass.AP(part.tensor, part.offset, [list(part.ap[0]), [0, 4], [1, C]])
                    sp.dma_start(prev_rep[:, q, j, :], src).then_inc(prev_replicated[q], 16)

            sp.wait_ge(xt_staged, 1)
            write_xt(0, 0)
            sp.wait_ge(xt_written, 32)
            load_l0(0)
            load_l0(CH, first_xb, first_xm, first_x16, l0_chunk_1_loaded)
            load_xa(0, 0)
            sp.wait_ge(xt_staged, 2)
            write_xt(0, 1)
            load_xa(CH, 1)
            sp.wait_ge(l0_evacuated, 1)
            replicate_prev(0)

            def two_chunks(it, next_bt=None, last=False):
                value = int if last else work_out
                if next_bt is not None:
                    first = next_bt * (CPB * CH)
                    staged, written = value(2 * next_bt + 2), value(64 * next_bt + 64)
                for par in range(2):
                    c = 2 * it + par
                    next_but_one = (c + 2) * CH
                    c_plus_2, prev_copies = value(c + 2), value(J * c + 1)
                    wholes, wholes_after = value(L1_PAIRS * c + 1), value(L1_PAIRS * (c + 1))
                    products_after = value(split_base(c) + L1_PAIRS)
                    if not last:
                        sp.wait_ge(small_ready, c_plus_2)
                        load_l0(next_but_one)
                    if not (last and par):
                        sp.wait_ge(l0_evacuated, c_plus_2)
                        sp.wait_ge(prev_in_psum, prev_copies)
                        sp.wait_ge(whole_ready, wholes)
                        replicate_prev(1 - par)
                    if not last:
                        sp.wait_ge(product_ready, products_after)
                        sp.wait_ge(whole_ready, wholes_after)
                        load_xa(next_but_one, par)
                if next_bt is not None:
                    sp.wait_ge(xt_staged, staged)
                    write_xt(first, 0)
                    write_xt(first, 1)
                    sp.wait_ge(xt_written, written)

            loop_chunks(sp, two_chunks, load_ids)
            two_chunks(CHUNKS // 2 - 1, last=True)

            sp.wait_ge(y_ready, 1)
            sp.dma_start(out.rearrange("b o -> o b"), y).then_inc(y_written, 16)
            sp.wait_ge(y_written, 16)

        @block.gpsimd
        def _(pool):
            def gather(fields, done=gathered):
                for f in fields:
                    pool.indirect_dma_start(
                        emb[:, D * f:D * (f + 1)], None, tables[f],
                        bass.IndirectOffsetOnAxis(ap=idx[:, f:f + 1], axis=0)).then_inc(done, 16)

            pool.wait_ge(ids_loaded, 16)
            gather(range(EARLY), gathered_first)
            gather(range(EARLY, F))
            pool.memset(sum0[:], 0.0).then_inc(summed0, 1)
            pool.memset(half_sum[:, 0, :], 0.0).then_inc(folded0, 1)
            pool.memset(sum1[:], 0.0).then_inc(summed1, 2)

            def fold(which, total, summed, count, folded, before, dst):
                pool.wait_ge(summed, count)
                pool.tensor_tensor(half_sum[:, which, :], total[:, 0:2 * P], total[:, 2 * P:C],
                                   ALU.add).then_inc(folded, 1)
                pool.wait_ge(folded, before + 1)
                pool.tensor_tensor(dst, half_sum[:, which, 0:P], half_sum[:, which, P:2 * P],
                                   ALU.add).then_inc(folded, 1)

            GATHER_STEPS = 4 * L1_PAIRS + L1_PAIRS // 2

            def chunk(bt, dg, gathers):
                c = bt * CPB + dg
                par = dg % 2
                for k in range(L1_PAIRS):
                    j, g = k // (GS // 2), GS + 2 * (k % (GS // 2))
                    if k == 0:
                        pool.wait_ge(xa_loaded[par], 16 * (bt * (CPB // 2) + dg // 2 + 1))
                        pool.wait_ge(prev_replicated[par], 16 * J * (bt * (CPB // 2) + dg // 2 + 1))
                    pool.wait_ge(whole_free, L1_PAIRS * c + k + 1)
                    pool.tensor_tensor(
                        whole[:, k % R], xa[:, par, g:g + 2, :],
                        prev_rep[:, par, j, None, :].to_broadcast([P, 2, C]), ALU.mult).then_inc(whole_ready, 1)
                    if gathers and dg * L1_PAIRS + k < GATHER_STEPS:
                        step = dg * L1_PAIRS + k
                        gather(range(F * step // GATHER_STEPS, F * (step + 1) // GATHER_STEPS))
                    if k == 2 and dg != 1:
                        pool.wait_ge(l1_evacuated, c + 1)
                        if dg == 2:
                            pool.wait_ge(folded1, 2 * bt + 2)
                            pool.tensor_tensor(sum1[:], relu1[:, 0, :], relu1[:, 1, :], ALU.add).then_inc(summed1, 2)
                        else:
                            pool.wait_ge(summed1, c + 2)
                            pool.tensor_tensor(sum1[:], sum1[:], relu1[:, par, :], ALU.add).then_inc(summed1, 1)
                        if dg == 0:
                            fold(1, sum1, summed1, c + 3, folded1, 2 * bt, pooled1[:, bt, :])
                    if k == 5 and dg != CPB - 1:
                        pool.wait_ge(l0_evacuated, c + 2)
                        if dg == 0:
                            pool.wait_ge(folded0, 2 * bt + 1)
                            pool.tensor_tensor(sum0[:], prev[:, 0, :], prev[:, 1, :], ALU.add).then_inc(summed0, 2)
                        else:
                            pool.wait_ge(summed0, c + 2)
                            pool.tensor_tensor(sum0[:], sum0[:], prev[:, 1 - par, :], ALU.add).then_inc(summed0, 1)
                        if dg == CPB - 2:
                            fold(0, sum0, summed0, c + 3, folded0, 2 * bt + 1, pooled0[:, bt, :])

            pool.wait_ge(small_ready, 2)
            with pool.Fori(0, BT - 1) as bt:
                pool.wait_ge(ids_loaded, 16 * (bt + 2))
                pool.wait_ge(sorted_d, bt + 2)
                for dg in range(CPB):
                    chunk(bt, dg, True)
            for dg in range(CPB):
                chunk(BT - 1, dg, False)

        @block.scalar
        def _(act):
            for r in range(2):
                act.dma_start(dram(w0_mm, r * F * N, [[2 * F * N, F], [1, F * N]]),
                              dram(filter_0, 0, [[F * N, F], [1, F * N]])).then_inc(w0_doubled, 16)
                act.dma_start(dram(w0_hh, r * F * F * N, [[F * N, F], [1, F * N]]),
                              dram(filter_0, 0, [[F * N, F], [1, F * N]])).then_inc(w0_doubled, 16)
            act.wait_ge(w0_doubled, 64)
            act.dma_start(w0_a[:], dram(w0_mm, 0, [[(2 * F + 1) * N, F], [KT * N, 4], [1, KT * N]])).then_inc(
                w0_loaded, 16)
            for t in range(KT):
                act.dma_start(w0_b[:, t, :], dram(w0_hh, t * F * N, [[(F + 1) * N, F], [KT * F * N, 4], [1, N]])
                              ).then_inc(w0_loaded, 16)
            for r in range(3):
                act.dma_start(w16[F * r:F * (r + 1)], dram(w0_mm, 16 * N, [[(2 * F + 1) * N, F], [1, N]])).then_inc(
                    w0_loaded, 16)
            act.dma_start(wt1_sb[:], W_top1[0:2 * P, :].rearrange("(t p) n -> p t n", p=P)).then_inc(tower_loaded, 16)
            act.dma_start(wt1_ctx[:], W_top1[2 * N:2 * N + D_CTX, :]).then_inc(tower_loaded, 16)
            act.dma_start(wt2_sb[:], W_top2.rearrange("(t p) n -> p t n", p=P)).then_inc(tower_loaded, 16)
            with nc.allow_non_contiguous_dma(reason="a few hundred words, once"):
                act.dma_start(wt3_sb[:], W_top3.rearrange("(t p) n -> p (t n)", p=P)).then_inc(tower_loaded, 16)
                act.dma_start(bt1_sb[:], b_top1.rearrange("(t p) -> p t", p=P)).then_inc(tower_loaded, 16)
                act.dma_start(bt2_sb[:], b_top2.rearrange("(t p) -> p t", p=P)).then_inc(tower_loaded, 16)

            act.wait_ge(w0_loaded, 16 * (KT + 4))
            act.activation(w16_split[:], w16[:], ACT.Copy).then_inc(w_hi_ready, 1)
            act.wait_ge(w0_folded, 2)
            act.activation(w0_hi[:], w0_a[:], ACT.Copy).then_inc(w_hi_ready, 1)
            act.wait_ge(w1_loaded, 16 * J * G)
            act.activation(w1_hi[:], w1_raw[:], ACT.Copy).then_inc(w_hi_ready, 1)

            act.wait_ge(ctx_turned, 1)
            act.activation(ctx_t[:], acc0[0:D_CTX, :], ACT.Copy).then_inc(ctx_ready, 1)

            def sort_d(fields):
                act.activation(emb_sorted[:, :, DC * fields.start:DC * fields.stop].rearrange("b g (h d) -> b g h d", d=DC),
                               emb[:, D * fields.start:D * fields.stop].rearrange("b (h g d) -> b g h d", g=CPB, d=DC),
                               ACT.Copy).then_inc(sorted_d, 1)

            def stage_xt(half, src):
                act.activation(xt_stage[:, 4 * half:4 * half + 4, :], src, ACT.Copy).then_inc(xt_staged, 1)

            def split_high(n, slot):
                act.wait_ge(product_ready, n + 1)
                act.activation(hi[:, slot % R], prod[:, slot % 2], ACT.Copy).then_inc(hi_ready, 1)

            def small_high(c):
                act.wait_ge(small_ready, c + 1)
                act.activation(small_split[:], small[:], ACT.Copy).then_inc(small_hi_ready, 1)

            def relu_l0(c, q):
                act.wait_ge(l0_done, c + 1)
                act.activation(prev[:, q, :], acc0[:], ACT.Relu).then_inc(l0_evacuated, 1)

            act.wait_ge(gathered_first, 16 * EARLY)
            sort_d(slice(0, EARLY))
            act.wait_ge(gathered, 16 * (F - EARLY))
            sort_d(slice(EARLY, F))
            for half in range(2):
                act.wait_ge(transposed, half + 1)
                stage_xt(half, prod[:, half, 0, :])

            split_high(0, 0)
            split_high(1, 1)
            small_high(0)
            split_high(2, 2)
            relu_l0(0, 0)
            split_high(3, 3)
            act.wait_ge(small_lo_ready, 1)
            act.wait_ge(l0_done, 1)
            small_high(1)
            act.wait_ge(prev_replicated[0], 16 * J)
            act.activation(prev_ps[:, 0, :], prev_rep[:, 0, 0, :], ACT.Copy).then_inc(prev_in_psum, 1)

            def chunk(it, par, base, last, next_bt=None):
                c = 2 * it + par
                b0 = PAIRS * par if not last else (PAIRS * 0 if par == 0 else L1_PAIRS)
                for k in range(L1_PAIRS):
                    if k % 2 == 0:
                        j = k // 2 + 1
                        if j < J:
                            act.wait_ge(product_ready, base + k if k else base - L0_PAIRS)
                            act.activation(prev_ps[:, j % 2, :], prev_rep[:, par, j, :], ACT.Copy).then_inc(
                                prev_in_psum, 1)
                        elif not (last and par):
                            act.wait_ge(product_ready, base + k)
                            act.wait_ge(prev_replicated[1 - par], 16 * J * (it + 1 + par))
                            act.activation(prev_ps[:, 0, :], prev_rep[:, 1 - par, 0, :], ACT.Copy).then_inc(
                                prev_in_psum, 1)
                    act.wait_ge(split_used, base + k - R + 1)
                    split_high(base + k, b0 + k)
                    if k == 1:
                        act.wait_ge(l1_cleared, 1)
                        act.wait_ge(whole_free, L1_PAIRS * c + R)
                        act.wait_ge(summed1, c + 1)
                        act.activation(relu1[:, par, :], acc1[:], ACT.Relu).then_inc(l1_evacuated, 1)
                    if k == 3 and not (last and par):
                        act.wait_ge(summed0, c + 1)
                        relu_l0(c + 1, 1 - par)
                    if k == 2 and next_bt is not None:
                        act.wait_ge(gathered, 16 * F * next_bt + 16 * (F - EARLY))
                        act.wait_ge(transposed, 2 * next_bt)
                        sort_d(slice(0, F))
                    if k == 6 and next_bt is not None:
                        act.wait_ge(transposed, 2 * next_bt + 1)
                        act.wait_ge(xt_written, 64 * next_bt)
                        stage_xt(0, acc0[:])
                if not last:
                    for k in range(L1_PAIRS, PAIRS):
                        act.wait_ge(split_used, base + k - R + 1)
                        split_high(base + k, b0 + k)
                        if k == L1_PAIRS and next_bt is not None:
                            act.wait_ge(transposed, 2 * next_bt + 2)
                            stage_xt(1, acc0[:])
                    act.wait_ge(l0_done, c + 2)
                    small_high(c + 2)

            def two_chunks(it, next_bt=None):
                for par in range(2):
                    chunk(it, par, split_base(2 * it + par), False, next_bt if par else None)

            loop_chunks(act, two_chunks)
            chunk(CHUNKS // 2 - 1, 0, split_base(CHUNKS - 2), True)
            chunk(CHUNKS // 2 - 1, 1, LAST_BASE, True)
            act.wait_ge(whole_free, L1_PAIRS * CHUNKS + R)
            act.wait_ge(summed1, CHUNKS + 1)
            act.activation(relu1[:, 0, :], acc1[:], ACT.Relu).then_inc(l1_evacuated, 1)

            act.wait_ge(tower_loaded, 16 * 6)
            for q in range(H1 // P):
                act.wait_ge(tower_mm, q + 1)
                act.activation(h1[:, q, :], prod[:, q // 2, q % 2, :], ACT.Relu,
                               bias=bt1_sb[:, q:q + 1]).then_inc(tower_relu, 1)
            act.wait_ge(tower_mm, H1 // P + H2 // P)
            for q in range(H2 // P):
                act.activation(h2[:, q, :], prev_ps[:, q, :], ACT.Relu,
                               bias=bt2_sb[:, q:q + 1]).then_inc(tower_relu, 1)
            act.wait_ge(tower_mm, H1 // P + H2 // P + 1)
            act.activation(y, acc0[0:1, :], ACT.Copy).then_inc(y_ready, 1)

        @block.vector
        def _(dve):
            dve.memset(acc1[:], 0.0).then_inc(l1_cleared, 1)
            dve.wait_ge(consts_loaded, 48)
            dve.wait_ge(w0_loaded, 16 * (4 + KT))
            dve.tensor_tensor(w0_a[:], w0_a[:], w0_b[:], ALU.add).then_inc(w0_folded, 1)
            dve.wait_ge(w0_folded, 1)
            dve.tensor_scalar(w0_a[:, 0, :], w0_a[:, 0, :], halves[:, 0:1], None, ALU.mult).then_inc(w0_folded, 1)
            dve.wait_ge(w0_folded, 2)
            dve.wait_ge(w_hi_ready, 2)
            dve.tensor_tensor(w0_lo[:], w0_a[:], w0_hi[:].bitcast(F32), ALU.subtract).then_inc(w_lo_ready, 1)
            low_third = w16_split[2 * F:3 * F]
            dve.tensor_tensor(low_third, w16[2 * F:3 * F], low_third.bitcast(F32), ALU.subtract).then_inc(w_lo_ready, 1)
            dve.wait_ge(w_hi_ready, 3)
            dve.tensor_tensor(w1_lo[:], w1_raw[:], w1_hi[:].bitcast(F32), ALU.subtract).then_inc(w_lo_ready, 1)

            def low(n, slot):
                dve.wait_ge(hi_ready, n + 1)
                dve.tensor_tensor(lo[:, slot % R], prod[:, slot % 2], hi[:, slot % R].bitcast(F32),
                                  ALU.subtract).then_inc(lo_ready, 1)

            def product_l0(t, slot, x_b=xb[:], x_m=xm[:]):
                dve.tensor_tensor(prod[:, slot % 2], x_b[:, 2 * t:2 * t + 2, :],
                                  x_m[:, None, :].to_broadcast([P, 2, C]), ALU.mult).then_inc(product_ready, 1)

            def small_product(x_16=x16[:]):
                dve.tensor_tensor(small[:], x_16[:, 0, :], x_16[:, 1, :], ALU.mult).then_inc(small_ready, 1)

            def small_low(c):
                dve.wait_ge(small_hi_ready, c + 1)
                low_third = small_split[F:2 * F]
                dve.tensor_tensor(low_third, small[F:2 * F], low_third.bitcast(F32),
                                  ALU.subtract).then_inc(small_lo_ready, 1)

            dve.wait_ge(xt_staged, 2)
            dve.wait_ge(l0_loaded, 64)
            product_l0(0, 0)
            product_l0(1, 1)
            small_product()
            low(0, 0)
            low(1, 1)
            small_low(0)
            dve.wait_ge(l0_chunk_1_loaded, 64)
            dve.wait_ge(lo_ready, 2)
            product_l0(0, 2, first_xb, first_xm)
            product_l0(1, 3, first_xb, first_xm)
            dve.wait_ge(small_lo_ready, 1)
            small_product(first_x16)
            low(2, 2)
            low(3, 3)
            small_low(1)

            def chunk(it, par, base, last):
                c = 2 * it + par
                b0 = PAIRS * par if not last else (PAIRS * 0 if par == 0 else L1_PAIRS)
                pairs = L1_PAIRS if last else PAIRS
                dve.wait_ge(xa_loaded[par], 16 * (it + 1))
                for k in range(pairs):
                    dve.wait_ge(lo_ready, base + k - 1)
                    if k < L1_PAIRS:
                        j, g = k // 2, 2 * (k % 2)
                        if k % 2 == 0:
                            dve.wait_ge(prev_in_psum, J * c + j + 1)
                        dve.tensor_tensor(prod[:, (b0 + k) % 2], xa[:, par, g:g + 2, :],
                                          prev_ps[:, j % 2, None, :].to_broadcast([P, 2, C]),
                                          ALU.mult).then_inc(product_ready, 1)
                    else:
                        if k == L1_PAIRS:
                            dve.wait_ge(l0_loaded, 64 * (c + 2))
                        product_l0(k - L1_PAIRS, b0 + k)
                    if k:
                        dve.wait_ge(split_used, base + k - R)
                        low(base + k - 1, b0 + k - 1)
                if not last:
                    dve.wait_ge(small_lo_ready, c + 2)
                    small_product()
                dve.wait_ge(split_used, base + pairs - R)
                low(base + pairs - 1, b0 + pairs - 1)
                if not last:
                    small_low(c + 2)

            with dve.Fori(0, CHUNKS // 2 - 1) as it:
                for par in range(2):
                    chunk(it, par, split_base(2 * it + par), False)
            chunk(CHUNKS // 2 - 1, 0, split_base(CHUNKS - 2), True)
            chunk(CHUNKS // 2 - 1, 1, LAST_BASE, True)

            dve.wait_ge(l1_evacuated, CHUNKS + 1)
            dve.wait_ge(summed1, CHUNKS + 2)
            dve.tensor_tensor(sum1[:], sum1[:], relu1[:, 0, :], ALU.add).then_inc(summed1, 1)
            dve.wait_ge(summed1, CHUNKS + 3)
            dve.tensor_tensor(half_sum[:, 1, :], sum1[:, 0:2 * P], sum1[:, 2 * P:C], ALU.add).then_inc(folded1, 1)
            dve.wait_ge(folded1, 2 * BT + 1)
            dve.tensor_tensor(pooled1[:, BT, :], half_sum[:, 1, 0:P], half_sum[:, 1, P:2 * P],
                              ALU.add).then_inc(folded1, 1)

        @block.tensor
        def _(pe):
            pe.sem_inc(whole_free, R)
            pe.wait_ge(consts_loaded, 48)
            for t in range(BT):
                turn = pe.transpose(acc0[0:D_CTX, P * t:P * (t + 1)], ctx_in[:, t, :], identity[:])
            turn.then_inc(ctx_turned, 1)
            pe.wait_ge(ctx_ready, 1)

            def transpose_x(dst, half):
                for q in range(4):
                    turn = pe.transpose(dst[:, P * q:P * (q + 1)], emb_sorted[:, 4 * half + q, :], identity[:])
                turn.then_inc(transposed, 1)

            def three_passes(acc, w_hi, w_lo, v_hi, v_lo, start, stop):
                pe.matmul(acc, w_hi, v_hi, start=start, stop=False)
                pe.matmul(acc, w_hi, v_lo, start=False, stop=False)
                return pe.matmul(acc, w_lo, v_hi, start=False, stop=stop)

            def layer0(c, n, slot):
                for t in range(KT):
                    if t % 2 == 0:
                        pe.wait_ge(lo_ready, n + t // 2 + 1)
                    s = (slot + t // 2) % R
                    mm = three_passes(acc0[:], w0_hi[:, t, :], w0_lo[:, t, :], hi[:, s, t % 2, :],
                                      lo[:, s, t % 2, :], t == 0, False)
                    if t % 2 == 1:
                        mm.then_inc(split_used, 1)
                pe.wait_ge(small_lo_ready, c + 1)
                pe.matmul(acc0[:], w16_split[:], small_split[:], start=False, stop=True).then_inc(l0_done, 1)

            pe.wait_ge(sorted_d, 2)
            for half in range(2):
                transpose_x(prod[:, half, 0, :], half)
            pe.wait_ge(w_lo_ready, 3)
            layer0(0, 0, 0)
            pe.wait_ge(l0_evacuated, 1)
            layer0(1, L0_PAIRS, L0_PAIRS)

            def chunk(it, par, base, last, next_bt=None):
                c = 2 * it + par
                b0 = PAIRS * par if not last else (PAIRS * 0 if par == 0 else L1_PAIRS)
                pe.wait_ge(l1_evacuated, c + 1)
                for k in range(L1_PAIRS):
                    j, g = k // 2, 2 * (k % 2)
                    s = (b0 + k) % R
                    pe.wait_ge(lo_ready, base + k + 1)
                    for u in range(2):
                        mm = three_passes(acc1[:], w1_hi[:, j, g + u, :], w1_lo[:, j, g + u, :],
                                          hi[:, s, u, :], lo[:, s, u, :], k == 0 and u == 0, False)
                    mm.then_inc(split_used, 1)
                    pe.wait_ge(whole_ready, L1_PAIRS * c + k + 1)
                    for u in range(2):
                        mm = pe.matmul(acc1[:], w1_whole[:, j, g + u, :], whole[:, k % R, u, :],
                                       start=False, stop=k == L1_PAIRS - 1 and u == 1)
                    mm.then_inc(whole_free, 1)
                    if k == 1 and next_bt is not None:
                        pe.wait_ge(l0_evacuated, c + 2)
                        pe.wait_ge(sorted_d, next_bt + 2)
                        transpose_x(acc0, 0)
                    if k == 4 and next_bt is not None:
                        pe.wait_ge(xt_staged, 2 * next_bt + 1)
                        transpose_x(acc0, 1)
                if not last:
                    pe.wait_ge(l0_evacuated, c + 2)
                    if next_bt is not None:
                        pe.wait_ge(xt_staged, 2 * next_bt + 2)
                    layer0(c + 2, base + L1_PAIRS, b0 + L1_PAIRS)

            def two_chunks(it, next_bt=None):
                for par in range(2):
                    chunk(it, par, split_base(2 * it + par), False, next_bt if par else None)

            loop_chunks(pe, two_chunks)
            chunk(CHUNKS // 2 - 1, 0, split_base(CHUNKS - 2), True)
            chunk(CHUNKS // 2 - 1, 1, LAST_BASE, True)

            pe.wait_ge(tower_loaded, 16 * 6)
            pe.wait_ge(folded0, 2 * BT + 1)
            for q in range(H1 // P):
                pe.matmul(prod[:, q // 2, q % 2, :], wt1_sb[:, 0, P * q:P * (q + 1)], pooled0[:], start=True, stop=False)
                pe.matmul(prod[:, q // 2, q % 2, :], wt1_ctx[:, P * q:P * (q + 1)], ctx_t[:], start=False, stop=False)
            pe.wait_ge(folded1, 2 * BT + 2)
            for q in range(H1 // P):
                pe.matmul(prod[:, q // 2, q % 2, :], wt1_sb[:, 1, P * q:P * (q + 1)], pooled1[:, 1:BT + 1, :],
                          start=False, stop=True).then_inc(tower_mm, 1)
            for t in range(H1 // P):
                pe.wait_ge(tower_relu, t + 1)
                for q in range(H2 // P):
                    mm = pe.matmul(prev_ps[:, q, :], wt2_sb[:, t, P * q:P * (q + 1)], h1[:, t, :],
                                   start=t == 0, stop=t == H1 // P - 1)
                    if t == H1 // P - 1:
                        mm.then_inc(tower_mm, 1)
            for t in range(H2 // P):
                pe.wait_ge(tower_relu, H1 // P + t + 1)
                mm = pe.matmul(acc0[0:1, :], wt3_sb[:, t:t + 1], h2[:, t, :], start=t == 0, stop=t == H2 // P - 1)
            mm.then_inc(tower_mm, 1)


def kernel(**inputs):
    import numpy as np
    import concourse.bacc as bacc
    from concourse.bass_utils import run_bass_kernel_spmd

    nc = bacc.Bacc("TRN2", target_bir_lowering=False, num_devices=1)
    arrays = {}

    def given(name, a):
        arrays[f"in_{name}"] = np.ascontiguousarray(a)
        a = arrays[f"in_{name}"]
        return nc.dram_tensor(f"in_{name}", a.shape, mybir.dt.from_np(a.dtype), kind="ExternalInput").ap()

    n_fields = inputs["ids"].shape[1]
    scale = np.ones((P, 1), np.float32)
    scale[::4] = 0.5
    args = [given("dense_ctx", inputs["dense_ctx"]), given("ids", inputs["ids"]),
            [given(f"tbl_{f}", inputs[f"tbl_{f}"]) for f in range(n_fields)]]
    args += [given(n, inputs[n]) for n in ("W_top1", "b_top1", "W_top2", "b_top2", "W_top3",
                                           "L0_rec_filter_0", "L0_rec_filter_1")]
    args += [given("eye", np.eye(P, dtype=np.float32)), given("fold_scale", scale)]
    y = nc.dram_tensor("y", (inputs["ids"].shape[0], 1), F32, kind="ExternalOutput").ap()
    cin_tower(nc, *args, y)
    r = run_bass_kernel_spmd(nc, [arrays], core_ids=[0])
    return r.results[0]["y"]
```

```python
from contextlib import ExitStack

import concourse.bass as bass
from concourse import mybir

ALU = mybir.AluOpType
ACT = mybir.ActivationFunctionType
F32 = mybir.dt.float32
F32R = mybir.dt.float32r
I32 = mybir.dt.int32

P = 128
N_IN_FLIGHT = 4


def cin_tower(nc, dense_ctx, ids, tables, W_top1, b_top1, W_top2, b_top2, W_top3,
              filter_0, filter_1, eye, fold_scale, out):
    B, D_CTX = dense_ctx.shape
    F = ids.shape[1]
    D = tables[0].shape[1]
    N = filter_0.shape[2]
    H1 = W_top1.shape[1]
    H2 = W_top2.shape[1]
    BT = B // P
    DC = 4
    C = DC * P
    CPB = D // DC
    CHUNKS = BT * CPB
    ROWS = F + 16
    KT = 4
    J = N // 32
    G = F // 4
    SPLIT = [(j, g) for j in range(J) for g in (0, 2)] + [(J - 1, 4)]
    WHOLE = [(j, g) for j in range(J) for g in (4, 6) if (j, g) not in SPLIT]
    WHOLE_AFTER = [0, 1, 3, 4, 5, 7, 8]
    L1_PAIRS = len(SPLIT)
    WHOLES = len(WHOLE)
    L0_PAIRS = KT // 2
    PAIRS = L1_PAIRS + L0_PAIRS
    EARLY = 3 * F // 4
    L0_PARTS = 16
    HEAD = 10
    R = N_IN_FLIGHT
    assert (F, D, N, B % P) == (32, 32, 128, 0)
    assert R == 4 and 2 * PAIRS == 22 and WHOLES == len(WHOLE_AFTER) == 7
    SLOTS = [0, 1, 2, 3, 4] * 2 + [0, 1, 2, 3] * 3
    FIRST_SLOTS = [0, 1, 2, 3]

    xt = nc.dram_tensor("xt_scratch", (CHUNKS, ROWS, C), F32).ap()
    w0_mm = nc.dram_tensor("w0_second_index_twice", (F, 2 * F, N), F32).ap()
    w0_hh = nc.dram_tensor("w0_first_index_twice", (2 * F, F, N), F32).ap()
    CH = ROWS * C

    with ExitStack() as ctx:
        def sb(name, shape, dt=F32):
            return ctx.enter_context(nc.sbuf_tensor(name, shape, dt))

        def psum(name, shape):
            return ctx.enter_context(nc.psum_tensor(name, shape, F32))

        def sem(name):
            return ctx.enter_context(nc.semaphore(name))

        acc0 = psum("acc0", [P, C])
        acc1 = psum("acc1", [P, C])
        prev_ps = psum("prev_ps", [P, 2, C])
        prod = psum("prod", [P, 2, 2, C])

        identity = sb("identity", [P, P])
        halves = sb("halves", [P, 1])
        idx = sb("idx", [P, F], I32)
        idx_head = sb("idx_head", [P, HEAD], I32)
        idx_tail = sb("idx_tail", [P, F - HEAD], I32)
        emb = sb("emb", [P, F * D])
        emb_sorted = sb("emb_sorted", [P, CPB, F * DC])
        xt_stage = sb("xt_stage", [P, CPB, P])

        xa = sb("xa", [P, 2, G, C])
        xb = sb("xb", [P, KT, C])
        xm = sb("xm", [P, C])
        x16 = sb("x16", [3 * F, 2, C])
        prev = sb("prev", [P, 2, C])
        prev_rep = sb("prev_rep", [P, 2, J, C])
        relu1 = sb("relu1", [P, 2, C])
        hi = sb("hi", [P, R + 1, 2, C], F32R)
        lo = sb("lo", [P, R + 1, 2, C], F32R)
        whole = sb("whole", [P, R, 2, C])
        small = sb("small", [3 * F, C])
        small_split = sb("small_split", [3 * F, C], F32R)

        w1_raw = whole[:].rearrange("p r u c -> p (r u c)")[:, 0:L1_PAIRS * 2 * N].rearrange(
            "p (k u n) -> p k u n", k=L1_PAIRS, u=2)
        w1_hi = sb("w1_hi", [P, L1_PAIRS, 2, N], F32R)
        w1_lo = sb("w1_lo", [P, L1_PAIRS, 2, N], F32R)
        w1_whole = sb("w1_whole", [P, WHOLES, 2, N])
        w0_a = sb("w0_a", [P, KT, N])
        w0_b = sb("w0_b", [P, KT, N])
        w0_hi = sb("w0_hi", [P, KT, N], F32R)
        w0_lo = sb("w0_lo", [P, KT, N], F32R)
        w16 = sb("w16", [3 * F, N])
        w16_split = sb("w16_split", [3 * F, N], F32R)

        sum0 = sb("sum0", [P, C])
        sum1 = sb("sum1", [P, C])
        half_sum = sb("half_sum", [P, 2, 2 * P])
        pooled0 = sb("pooled0", [P, BT, P])
        pooled1 = sb("pooled1", [P, BT + 1, P])
        ctx_in = sb("ctx_in", [P, BT, D_CTX])
        ctx_t = sb("ctx_t", [D_CTX, B])
        ctx_share = sb("ctx_share", [P, H1 // P, B])
        wt1_sb = sb("wt1_sb", [P, 2, H1])
        wt1_ctx = sb("wt1_ctx", [D_CTX, H1])
        wt2_sb = sb("wt2_sb", [P, H1 // P, H2])
        wt3_sb = sb("wt3_sb", [P, H2 // P])
        bt1_sb = sb("bt1_sb", [P, H1 // P])
        bt2_sb = sb("bt2_sb", [P, H2 // P])
        h1 = xa[:, 0, 0:H1 // P, :]
        h1_sum = xa[:, 0, H1 // P:2 * H1 // P, :]
        h2 = xa[:, 1, 0:H2 // P, :]
        y = small[0:1, :]
        first_xb = prev_rep[:, 1]
        first_xm = relu1[:, 1, :]
        first_x16 = whole[0:3 * F, R - 1]

        ids_loaded = sem("ids_loaded")
        heads_loaded = sem("heads_loaded")
        tails_loaded = sem("tails_loaded")
        consts_loaded = sem("consts_loaded")
        w0_doubled = sem("w0_doubled")
        w0_loaded = sem("w0_loaded")
        w1_loaded = sem("w1_loaded")
        tower_loaded = sem("tower_loaded")
        w0_folded = sem("w0_folded")
        w_hi_ready = sem("w_hi_ready")
        w_lo_ready = sem("w_lo_ready")
        gathered_first = sem("gathered_first")
        gathered = sem("gathered")
        sorted_d = sem("sorted_d")
        transposed = sem("transposed")
        xt_staged = sem("xt_staged")
        xt_first_written = sem("xt_first_written")
        xt_written = sem("xt_written")
        l0_loaded = sem("l0_loaded")
        l0_first_pair_loaded = sem("l0_first_pair_loaded")
        l0_first_small_loaded = sem("l0_first_small_loaded")
        l0_chunk_1_loaded = sem("l0_chunk_1_loaded")
        xa_loaded = [sem(f"xa_loaded_{q}") for q in range(2)]
        prev_replicated = [[sem(f"prev_replicated_{q}_{j}") for j in range(J)] for q in range(2)]
        prev_in_psum = sem("prev_in_psum")
        product_ready = sem("product_ready")
        hi_ready = sem("hi_ready")
        lo_ready = sem("lo_ready")
        split_used = sem("split_used")
        small_ready = sem("small_ready")
        small_hi_ready = sem("small_hi_ready")
        small_lo_ready = sem("small_lo_ready")
        whole_ready = sem("whole_ready")
        whole_free = sem("whole_free")
        l0_done = sem("l0_done")
        l0_evacuated = sem("l0_evacuated")
        l1_cleared = sem("l1_cleared")
        l1_evacuated = sem("l1_evacuated")
        summed0 = sem("summed0")
        summed1 = sem("summed1")
        folded0 = sem("folded0")
        folded1 = sem("folded1")
        ctx_turned = sem("ctx_turned")
        ctx_ready = sem("ctx_ready")
        ctx_mm = sem("ctx_mm")
        ctx_share_ready = sem("ctx_share_ready")
        tower_sum = sem("tower_sum")
        tower_mm = sem("tower_mm")
        tower_relu = sem("tower_relu")
        y_ready = sem("y_ready")
        y_written = sem("y_written")

        def split_base(c):
            return 2 * L0_PAIRS + PAIRS * c

        LAST_BASE = split_base(CHUNKS - 2) + L1_PAIRS

        def slot_free(n, i):
            back = next(b for b in range(1, 23) if SLOTS[(i - b) % 22] == SLOTS[i])
            return n - min(back, 7) + 1

        def whole_slot_free(c, k):
            back = 3 if k < 3 else 7 if k == 3 else 4
            return WHOLES * c + (k - back + 1 + R)

        def loop_chunks(eng, body, begin=None):
            def batch_tile(bt):
                if begin:
                    begin(bt + 1)
                with eng.Fori(0, CPB // 2 - 2) as pair:
                    body(bt * (CPB // 2) + pair)
                body(bt * (CPB // 2) + (CPB // 2 - 2), bt + 1)
                body(bt * (CPB // 2) + (CPB // 2 - 1))

            looped = BT - 2 if begin else BT - 1
            with eng.Fori(0, looped) as bt:
                batch_tile(bt)
            if begin:
                batch_tile(BT - 2)
            with eng.Fori((BT - 1) * (CPB // 2), CHUNKS // 2 - 1) as half:
                body(half)

        def dram(tensor, offset, dims):
            return bass.AP(tensor.tensor, offset, dims)

        block = ctx.enter_context(nc.Block())

        @block.sync
        def _(sp):
            sp.dma_start(idx[:], ids[0:P, :]).then_inc(ids_loaded, 16)
            with nc.allow_non_contiguous_dma(reason="rows of a few ids"):
                sp.dma_start(idx_head[:], ids[P:2 * P, 0:HEAD]).then_inc(heads_loaded, 16)
            sp.dma_start(identity[:], eye).then_inc(consts_loaded, 16)
            sp.dma_start(halves[:], fold_scale).then_inc(consts_loaded, 16)
            sp.dma_start(ctx_in[:], dense_ctx.rearrange("(t p) f -> p t f", p=P)).then_inc(consts_loaded, 16)

            for w1, pairs in ((w1_raw, SPLIT), (w1_whole, WHOLE)):
                for k, (j, g) in enumerate(pairs):
                    for u in range(2):
                        src = dram(filter_1, ((g + u) * N + 32 * j) * N, [[N, 32], [G * N * N, 4], [1, N]])
                        sp.dma_start(w1[:, k, u, :], src).then_inc(w1_loaded, 16)

            def work_out(x):
                return x if isinstance(x, int) else sp.snap(sp.to_reg(x))

            def load_ids(bt):
                gathers = work_out(16 * F * bt + 16 * (HEAD - EARLY))
                tail_at, head_at = bt * (P * F) + HEAD, bt * (P * F) + P * F
                sp.wait_ge(gathered, gathers)
                with nc.allow_non_contiguous_dma(reason="rows of a few ids"):
                    sp.dma_start(idx_tail[:], dram(ids, tail_at, [[F, P], [1, F - HEAD]])).then_inc(tails_loaded, 16)
                    if not isinstance(bt, int):
                        sp.dma_start(idx_head[:], dram(ids, head_at, [[F, P], [1, HEAD]])).then_inc(heads_loaded, 16)

            def write_xt(first, start, stop, done=xt_written):
                at = first + start * CH
                part = xt_stage[:, start:stop, :]
                sp.dma_start(dram(xt, at, [[P, P], [CH, stop - start], [1, P]]), part).then_inc(done, 16)
                sp.dma_start(dram(xt, at + F * C, [[P, 64], [CH, stop - start], [1, P]]), part[0:64]).then_inc(done, 16)

            def load_l0(at, x_b=xb[:], x_m=xm[:], x_16=x16[:], done=l0_loaded):
                sp.dma_start(x_b, dram(xt, at, [[C, F], [KT * C, 4], [1, KT * C]])).then_inc(done, 16)
                sp.dma_start(x_m, dram(xt, at, [[C, F], [0, 4], [1, C]])).then_inc(done, 16)
                for s in range(2):
                    sp.dma_start(x_16[:, s, :], dram(xt, at + 16 * C * s, [[0, 3], [C, F], [1, C]])).then_inc(
                        done, 16)

            def load_xa(at, q):
                sp.dma_start(xa[:, q], dram(xt, at, [[0, 32], [G * C, 4], [1, G * C]])).then_inc(
                    xa_loaded[q], 16)

            def replicate_prev(q):
                for j in range(J):
                    part = prev[32 * j:32 * (j + 1), q, :]
                    src = bass.AP(part.tensor, part.offset, [list(part.ap[0]), [0, 4], [1, C]])
                    sp.dma_start(prev_rep[:, q, j, :], src).then_inc(prev_replicated[q][j], 16)

            sp.wait_ge(xt_staged, 1)
            write_xt(0, 0, 2, xt_first_written)
            sp.wait_ge(xt_first_written, 32)
            halves_of_xb = [dram(xt, 2 * C * t, [[C, F], [KT * C, 4], [1, 2 * C]]) for t in range(2)]
            sp.dma_start(xm[:], dram(xt, 0, [[C, F], [0, 4], [1, C]])).then_inc(l0_first_pair_loaded, 16)
            sp.dma_start(xb[:, 0:2, :], halves_of_xb[0]).then_inc(l0_first_pair_loaded, 16)
            sp.dma_start(xb[:, 2:4, :], halves_of_xb[1]).then_inc(l0_loaded, 16)
            for s in range(2):
                sp.dma_start(x16[:, s, :], dram(xt, 16 * C * s, [[0, 3], [C, F], [1, C]])).then_inc(
                    l0_first_small_loaded, 16)
            load_l0(CH, first_xb, first_xm, first_x16, l0_chunk_1_loaded)
            load_xa(0, 0)
            sp.wait_ge(l0_evacuated, 1)
            replicate_prev(0)
            sp.wait_ge(xt_staged, 2)
            write_xt(0, 2, 4)
            write_xt(0, 4, CPB)
            load_xa(CH, 1)
            sp.wait_ge(xt_written, 64)

            def two_chunks(it, next_bt=None, last=False):
                if next_bt is not None:
                    first = next_bt * (CPB * CH)
                    staged, written = work_out(2 * next_bt + 2), work_out(64 * next_bt + 64)
                for par in range(2):
                    c = 2 * it + par
                    next_but_one = (c + 2) * CH
                    c_plus_2, prev_copies = work_out(c + 2), work_out(J * c + 1)
                    wholes, wholes_after = work_out(WHOLES * c + 1), work_out(WHOLES * (c + 1))
                    products, products_after = work_out(split_base(c)), work_out(split_base(c) + L1_PAIRS)
                    if not last:
                        sp.wait_ge(product_ready, products)
                        sp.wait_ge(small_ready, c_plus_2)
                        load_l0(next_but_one)
                    if not (last and par):
                        sp.wait_ge(l0_evacuated, c_plus_2)
                        sp.wait_ge(prev_in_psum, prev_copies)
                        sp.wait_ge(whole_ready, wholes)
                        replicate_prev(1 - par)
                    if not last:
                        sp.wait_ge(product_ready, products_after)
                        sp.wait_ge(whole_ready, wholes_after)
                        load_xa(next_but_one, par)
                if next_bt is not None:
                    sp.wait_ge(xt_staged, staged)
                    write_xt(first, 0, 4)
                    write_xt(first, 4, CPB)
                    sp.wait_ge(xt_written, written)

            loop_chunks(sp, two_chunks, load_ids)
            two_chunks(CHUNKS // 2 - 1, last=True)

            sp.wait_ge(y_ready, 1)
            sp.dma_start(out.rearrange("b o -> o b"), y).then_inc(y_written, 16)
            sp.wait_ge(y_written, 16)

        @block.gpsimd
        def _(pool):
            def gather(fields, done=gathered, ids_of=lambda f: idx[:, f:f + 1]):
                for f in fields:
                    pool.indirect_dma_start(
                        emb[:, D * f:D * (f + 1)], None, tables[f],
                        bass.IndirectOffsetOnAxis(ap=ids_of(f), axis=0)).then_inc(done, 16)

            pool.wait_ge(ids_loaded, 16)
            gather(range(EARLY), gathered_first)
            gather(range(EARLY, F))
            pool.memset(sum0[:], 0.0).then_inc(summed0, 1)
            pool.memset(half_sum[:, 0, :], 0.0).then_inc(folded0, 1)
            pool.memset(sum1[:], 0.0).then_inc(summed1, 2)
            pool.wait_ge(heads_loaded, 16)
            pool.wait_ge(sorted_d, 2)

            def fold(which, total, summed, count, folded, before, dst):
                pool.wait_ge(summed, count)
                pool.tensor_tensor(half_sum[:, which, :], total[:, 0:2 * P], total[:, 2 * P:C],
                                   ALU.add).then_inc(folded, 1)
                pool.wait_ge(folded, before + 1)
                pool.tensor_tensor(dst, half_sum[:, which, 0:P], half_sum[:, which, P:2 * P],
                                   ALU.add).then_inc(folded, 1)

            def head_ids(f):
                return idx_head[:, f:f + 1]

            def tail_ids(f):
                return idx_tail[:, f - HEAD:f - HEAD + 1]

            TAIL_STEPS = range(3, 4 * WHOLES + WHOLES // 2)
            HEAD_STEPS = range(6 * WHOLES, 8 * WHOLES)

            def chunk(bt, dg, tail, head):
                c = bt * CPB + dg
                par = dg % 2
                for k, (j, g) in enumerate(WHOLE):
                    if k == 0:
                        pool.wait_ge(xa_loaded[par], 16 * (bt * (CPB // 2) + dg // 2 + 1))
                    if k == 0 or j != WHOLE[k - 1][0]:
                        pool.wait_ge(prev_replicated[par][j], 16 * (bt * (CPB // 2) + dg // 2 + 1))
                    pool.wait_ge(whole_free, whole_slot_free(c, k))
                    pool.tensor_tensor(
                        whole[:, k % R], xa[:, par, g:g + 2, :],
                        prev_rep[:, par, j, None, :].to_broadcast([P, 2, C]), ALU.mult).then_inc(whole_ready, 1)
                    step = dg * WHOLES + k
                    if tail and step in TAIL_STEPS:
                        n = step - TAIL_STEPS.start
                        if n == 0:
                            pool.wait_ge(tails_loaded, 16 * (bt + 1))
                        gather(range(HEAD + (F - HEAD) * n // len(TAIL_STEPS),
                                     HEAD + (F - HEAD) * (n + 1) // len(TAIL_STEPS)), ids_of=tail_ids)
                    if head and step in HEAD_STEPS:
                        n = step - HEAD_STEPS.start
                        gather(range(HEAD * n // len(HEAD_STEPS), HEAD * (n + 1) // len(HEAD_STEPS)), ids_of=head_ids)
                    if k == 2 and dg != 1:
                        pool.wait_ge(l1_evacuated, c + 1)
                        if dg == 2:
                            pool.wait_ge(folded1, 2 * bt + 2)
                            pool.tensor_tensor(sum1[:], relu1[:, 0, :], relu1[:, 1, :], ALU.add).then_inc(summed1, 2)
                        else:
                            pool.wait_ge(summed1, c + 2)
                            pool.tensor_tensor(sum1[:], sum1[:], relu1[:, par, :], ALU.add).then_inc(summed1, 1)
                        if dg == 0:
                            fold(1, sum1, summed1, c + 3, folded1, 2 * bt, pooled1[:, bt, :])
                    if k == 5 and (tail or head or bt != BT - 1 or dg < CPB - 2):
                        pool.wait_ge(l0_loaded, 64 * (c + 1) + L0_PARTS)
                        pool.wait_ge(small_lo_ready, c + 2)
                        pool.tensor_tensor(small[:], x16[:, 0, :], x16[:, 1, :], ALU.mult).then_inc(small_ready, 1)
                    if k == 4 and dg != CPB - 1:
                        pool.wait_ge(l0_evacuated, c + 2)
                        if dg == 0:
                            pool.wait_ge(folded0, 2 * bt + 1)
                            pool.tensor_tensor(sum0[:], prev[:, 0, :], prev[:, 1, :], ALU.add).then_inc(summed0, 2)
                        else:
                            pool.wait_ge(summed0, c + 2)
                            pool.tensor_tensor(sum0[:], sum0[:], prev[:, 1 - par, :], ALU.add).then_inc(summed0, 1)
                        if dg == CPB - 2:
                            fold(0, sum0, summed0, c + 3, folded0, 2 * bt + 1, pooled0[:, bt, :])

            gather(range(HEAD), ids_of=head_ids)
            pool.wait_ge(small_ready, 2)

            def batch_tile(bt, tail, head):
                for dg in range(CPB):
                    if head and dg == HEAD_STEPS.start // WHOLES:
                        pool.wait_ge(heads_loaded, 16 * (bt + 2))
                        pool.wait_ge(sorted_d, bt + 3)
                    chunk(bt, dg, tail, head)

            with pool.Fori(0, BT - 2) as bt:
                batch_tile(bt, True, True)
            batch_tile(BT - 2, True, False)
            batch_tile(BT - 1, False, False)

        @block.scalar
        def _(act):
            for r in range(2):
                act.dma_start(dram(w0_mm, r * F * N, [[2 * F * N, F], [1, F * N]]),
                              dram(filter_0, 0, [[F * N, F], [1, F * N]])).then_inc(w0_doubled, 16)
                act.dma_start(dram(w0_hh, r * F * F * N, [[F * N, F], [1, F * N]]),
                              dram(filter_0, 0, [[F * N, F], [1, F * N]])).then_inc(w0_doubled, 16)
            act.wait_ge(w0_doubled, 64)
            act.dma_start(w0_a[:], dram(w0_mm, 0, [[(2 * F + 1) * N, F], [KT * N, 4], [1, KT * N]])).then_inc(
                w0_loaded, 16)
            for t in range(KT):
                act.dma_start(w0_b[:, t, :], dram(w0_hh, t * F * N, [[(F + 1) * N, F], [KT * F * N, 4], [1, N]])
                              ).then_inc(w0_loaded, 16)
            for r in range(3):
                act.dma_start(w16[F * r:F * (r + 1)], dram(w0_mm, 16 * N, [[(2 * F + 1) * N, F], [1, N]])).then_inc(
                    w0_loaded, 16)
            act.dma_start(wt1_sb[:], W_top1[0:2 * P, :].rearrange("(t p) n -> p t n", p=P)).then_inc(tower_loaded, 16)
            act.dma_start(wt1_ctx[:], W_top1[2 * N:2 * N + D_CTX, :]).then_inc(tower_loaded, 16)
            act.dma_start(wt2_sb[:], W_top2.rearrange("(t p) n -> p t n", p=P)).then_inc(tower_loaded, 16)
            with nc.allow_non_contiguous_dma(reason="a few hundred words, once"):
                act.dma_start(wt3_sb[:], W_top3.rearrange("(t p) n -> p (t n)", p=P)).then_inc(tower_loaded, 16)
                act.dma_start(bt1_sb[:], b_top1.rearrange("(t p) -> p t", p=P)).then_inc(tower_loaded, 16)
                act.dma_start(bt2_sb[:], b_top2.rearrange("(t p) -> p t", p=P)).then_inc(tower_loaded, 16)

            act.wait_ge(w0_loaded, 16 * (KT + 4))
            act.activation(w16_split[:], w16[:], ACT.Copy).then_inc(w_hi_ready, 1)
            act.wait_ge(w0_folded, 2)
            act.activation(w0_hi[:], w0_a[:], ACT.Copy).then_inc(w_hi_ready, 1)
            act.wait_ge(w1_loaded, 16 * J * G)
            act.activation(w1_hi[:], w1_raw, ACT.Copy).then_inc(w_hi_ready, 1)

            act.wait_ge(ctx_turned, 1)
            act.activation(ctx_t[:], acc0[0:D_CTX, :], ACT.Copy).then_inc(ctx_ready, 1)

            def sort_d(fields):
                act.activation(emb_sorted[:, :, DC * fields.start:DC * fields.stop].rearrange("b g (h d) -> b g h d", d=DC),
                               emb[:, D * fields.start:D * fields.stop].rearrange("b (h g d) -> b g h d", g=CPB, d=DC),
                               ACT.Copy).then_inc(sorted_d, 1)

            def stage_xt(half, src):
                act.activation(xt_stage[:, 4 * half:4 * half + 4, :], src, ACT.Copy).then_inc(xt_staged, 1)

            def split_high(n, n_prod, slot):
                act.wait_ge(product_ready, n + 1)
                act.activation(hi[:, slot], prod[:, n_prod % 2], ACT.Copy).then_inc(hi_ready, 1)

            def small_high(c):
                act.wait_ge(small_ready, c + 1)
                act.activation(small_split[:], small[:], ACT.Copy).then_inc(small_hi_ready, 1)

            def relu_l0(c, q):
                act.wait_ge(l0_done, c + 1)
                act.activation(prev[:, q, :], acc0[:], ACT.Relu).then_inc(l0_evacuated, 1)

            act.wait_ge(gathered_first, 16 * EARLY)
            sort_d(slice(0, EARLY))
            act.wait_ge(gathered, 16 * (F - EARLY))
            sort_d(slice(EARLY, F))
            for half in range(2):
                act.wait_ge(transposed, half + 1)
                stage_xt(half, prod[:, half, 0, :])

            def copy_ctx_share(q):
                act.wait_ge(ctx_mm, q + 1)
                act.activation(ctx_share[:, q, :], prev_ps[:, q % 2, :], ACT.Identity,
                               bias=bt1_sb[:, q:q + 1]).then_inc(ctx_share_ready, 1)

            act.wait_ge(tower_loaded, 16 * 6)
            copy_ctx_share(0)
            copy_ctx_share(1)
            split_high(0, 0, FIRST_SLOTS[0])
            split_high(1, 1, FIRST_SLOTS[1])
            small_high(0)
            copy_ctx_share(2)
            copy_ctx_share(3)
            relu_l0(0, 0)
            split_high(2, 2, FIRST_SLOTS[2])
            split_high(3, 3, FIRST_SLOTS[3])
            act.wait_ge(small_lo_ready, 1)
            act.wait_ge(l0_done, 1)
            small_high(1)
            act.wait_ge(prev_replicated[0][0], 16)
            act.activation(prev_ps[:, 0, :], prev_rep[:, 0, 0, :], ACT.Copy).then_inc(prev_in_psum, 1)

            def chunk(it, par, base, last, next_bt=None):
                c = 2 * it + par
                b0 = par * (L1_PAIRS if last else PAIRS)
                odd = 1 - par

                def copy_prev(j):
                    act.wait_ge(prev_replicated[par][j], 16 * (it + 1))
                    act.activation(prev_ps[:, j % 2, :], prev_rep[:, par, j, :], ACT.Copy).then_inc(prev_in_psum, 1)

                if par == 0:
                    copy_prev(1)
                for k in range(L1_PAIRS if last else PAIRS):
                    act.wait_ge(split_used, slot_free(base + k, b0 + k))
                    split_high(base + k, b0 + k, SLOTS[b0 + k])
                    if k == 0 and par == 1:
                        copy_prev(1)
                    if k == odd:
                        act.wait_ge(l1_cleared, 1)
                        act.wait_ge(whole_free, WHOLES * c + R)
                        act.wait_ge(summed1, c + 1)
                        act.activation(relu1[:, par, :], acc1[:], ACT.Relu).then_inc(l1_evacuated, 1)
                    if k == 2 - odd:
                        copy_prev(2)
                    if k == 4 - odd:
                        copy_prev(3)
                    if k == 2 + odd:
                        if not (last and par):
                            act.wait_ge(summed0, c + 1)
                            relu_l0(c + 1, 1 - par)
                        if next_bt is not None:
                            act.wait_ge(gathered, 16 * F * next_bt + 16 * (F - EARLY))
                            act.wait_ge(transposed, 2 * next_bt)
                            sort_d(slice(0, F))
                    if k == 6 - odd and not (last and par):
                        act.wait_ge(prev_replicated[1 - par][0], 16 * (it + 1 + par))
                        act.activation(prev_ps[:, 0, :], prev_rep[:, 1 - par, 0, :], ACT.Copy).then_inc(prev_in_psum, 1)
                    if k == 6 and next_bt is not None:
                        act.wait_ge(transposed, 2 * next_bt + 1)
                        act.wait_ge(xt_written, 64 * next_bt)
                        stage_xt(0, acc0[:])
                    if k == PAIRS - 1 and next_bt is not None:
                        act.wait_ge(transposed, 2 * next_bt + 2)
                        stage_xt(1, acc0[:])
                if not last:
                    act.wait_ge(l0_done, c + 2)
                    small_high(c + 2)

            def two_chunks(it, next_bt=None):
                for par in range(2):
                    chunk(it, par, split_base(2 * it + par), False, next_bt if par else None)

            loop_chunks(act, two_chunks)
            chunk(CHUNKS // 2 - 1, 0, split_base(CHUNKS - 2), True)
            chunk(CHUNKS // 2 - 1, 1, LAST_BASE, True)
            act.wait_ge(whole_free, WHOLES * CHUNKS + R)
            act.wait_ge(summed1, CHUNKS + 1)
            act.activation(relu1[:, 0, :], acc1[:], ACT.Relu).then_inc(l1_evacuated, 1)

            for q in range(H1 // P):
                act.wait_ge(tower_sum, q + 1)
                act.activation(h1[:, q, :], h1_sum[:, q, :], ACT.Relu).then_inc(tower_relu, 1)
            act.wait_ge(tower_mm, H1 // P + H2 // P)
            for q in range(H2 // P):
                act.activation(h2[:, q, :], prev_ps[:, q, :], ACT.Relu,
                               bias=bt2_sb[:, q:q + 1]).then_inc(tower_relu, 1)
            act.wait_ge(tower_mm, H1 // P + H2 // P + 1)
            act.activation(y, acc0[0:1, :], ACT.Copy).then_inc(y_ready, 1)

        @block.vector
        def _(dve):
            dve.wait_ge(consts_loaded, 48)
            dve.wait_ge(w0_loaded, 16 * (4 + KT))
            dve.tensor_tensor(w0_a[:], w0_a[:], w0_b[:], ALU.add).then_inc(w0_folded, 1)
            dve.wait_ge(w0_folded, 1)
            dve.tensor_scalar(w0_a[:, 0, :], w0_a[:, 0, :], halves[:, 0:1], None, ALU.mult).then_inc(w0_folded, 1)
            dve.wait_ge(w0_folded, 2)
            dve.wait_ge(w_hi_ready, 2)
            dve.tensor_tensor(w0_lo[:], w0_a[:], w0_hi[:].bitcast(F32), ALU.subtract).then_inc(w_lo_ready, 1)
            low_third = w16_split[2 * F:3 * F]
            dve.tensor_tensor(low_third, w16[2 * F:3 * F], low_third.bitcast(F32), ALU.subtract).then_inc(w_lo_ready, 1)
            dve.wait_ge(w_hi_ready, 3)
            dve.tensor_tensor(w1_lo[:], w1_raw, w1_hi[:].bitcast(F32), ALU.subtract).then_inc(w_lo_ready, 1)

            def low(n, n_prod, slot):
                dve.wait_ge(hi_ready, n + 1)
                dve.tensor_tensor(lo[:, slot], prod[:, n_prod % 2], hi[:, slot].bitcast(F32),
                                  ALU.subtract).then_inc(lo_ready, 1)

            def product_l0(t, slot, x_b=xb[:], x_m=xm[:]):
                dve.tensor_tensor(prod[:, slot % 2], x_b[:, 2 * t:2 * t + 2, :],
                                  x_m[:, None, :].to_broadcast([P, 2, C]), ALU.mult).then_inc(product_ready, 1)

            def small_product(x_16=x16[:]):
                dve.tensor_tensor(small[:], x_16[:, 0, :], x_16[:, 1, :], ALU.mult).then_inc(small_ready, 1)

            def small_low(c):
                dve.wait_ge(small_hi_ready, c + 1)
                low_third = small_split[F:2 * F]
                dve.tensor_tensor(low_third, small[F:2 * F], low_third.bitcast(F32),
                                  ALU.subtract).then_inc(small_lo_ready, 1)

            dve.wait_ge(xt_staged, 2)
            dve.wait_ge(l0_first_pair_loaded, 32)
            product_l0(0, 0)
            dve.wait_ge(l0_loaded, L0_PARTS)
            product_l0(1, 1)
            dve.wait_ge(l0_first_small_loaded, 32)
            small_product()
            low(0, 0, FIRST_SLOTS[0])
            low(1, 1, FIRST_SLOTS[1])
            small_low(0)
            dve.wait_ge(l0_chunk_1_loaded, 64)
            dve.wait_ge(lo_ready, 2)
            product_l0(0, 2, first_xb, first_xm)
            product_l0(1, 3, first_xb, first_xm)
            dve.wait_ge(small_lo_ready, 1)
            small_product(first_x16)
            low(2, 2, FIRST_SLOTS[2])
            low(3, 3, FIRST_SLOTS[3])
            small_low(1)

            def product(it, par, k, n, i):
                c = 2 * it + par
                if k == 0:
                    dve.wait_ge(xa_loaded[par], 16 * (it + 1))
                if k == L1_PAIRS:
                    dve.wait_ge(l0_loaded, 64 * (c + 1) + L0_PARTS)
                dve.wait_ge(lo_ready, n - 1)
                if k < L1_PAIRS:
                    j, g = SPLIT[k]
                    if g == 0:
                        dve.wait_ge(prev_in_psum, J * c + j + 1)
                    dve.tensor_tensor(prod[:, i % 2], xa[:, par, g:g + 2, :],
                                      prev_ps[:, j % 2, None, :].to_broadcast([P, 2, C]),
                                      ALU.mult).then_inc(product_ready, 1)
                else:
                    product_l0(k - L1_PAIRS, i)

            def two_chunks(it, bases, pairs):
                steps = [(par, k) for par in range(2) for k in range(pairs)]
                for first in range(0, len(steps), 2):
                    for i in (first, first + 1):
                        par, k = steps[i]
                        product(it, par, k, bases[par] + k, i)
                    for i in (first, first + 1):
                        par, k = steps[i]
                        n = bases[par] + k
                        dve.wait_ge(split_used, slot_free(n, i))
                        low(n, i, SLOTS[i])
                        if k == PAIRS - 1:
                            small_low(2 * it + par + 2)

            with dve.Fori(0, CHUNKS // 2 - 1) as it:
                two_chunks(it, (split_base(2 * it), split_base(2 * it + 1)), PAIRS)
            two_chunks(CHUNKS // 2 - 1, (split_base(CHUNKS - 2), LAST_BASE), L1_PAIRS)

            dve.wait_ge(l1_evacuated, CHUNKS + 1)
            dve.wait_ge(summed1, CHUNKS + 2)
            dve.tensor_tensor(sum1[:], sum1[:], relu1[:, 0, :], ALU.add).then_inc(summed1, 1)
            dve.wait_ge(summed1, CHUNKS + 3)
            dve.tensor_tensor(half_sum[:, 1, :], sum1[:, 0:2 * P], sum1[:, 2 * P:C], ALU.add).then_inc(folded1, 1)
            dve.wait_ge(folded1, 2 * BT + 1)
            dve.tensor_tensor(pooled1[:, BT, :], half_sum[:, 1, 0:P], half_sum[:, 1, P:2 * P],
                              ALU.add).then_inc(folded1, 1)

            dve.wait_ge(ctx_share_ready, H1 // P)
            for q in range(H1 // P):
                dve.wait_ge(tower_mm, q + 1)
                dve.tensor_tensor(h1_sum[:, q, :], prod[:, q // 2, q % 2, :], ctx_share[:, q, :],
                                  ALU.add).then_inc(tower_sum, 1)

        @block.tensor
        def _(pe):
            pe.sem_inc(whole_free, R)
            pe.wait_ge(consts_loaded, 48)
            for t in range(BT):
                turn = pe.transpose(acc0[0:D_CTX, P * t:P * (t + 1)], ctx_in[:, t, :], identity[:])
            turn.then_inc(ctx_turned, 1)
            pe.wait_ge(ctx_ready, 1)

            def transpose_x(dst, half):
                for q in range(4):
                    turn = pe.transpose(dst[:, P * q:P * (q + 1)], emb_sorted[:, 4 * half + q, :], identity[:])
                turn.then_inc(transposed, 1)

            def three_passes(acc, w_hi, w_lo, v_hi, v_lo, start, stop):
                pe.matmul(acc, w_hi, v_hi, start=start, stop=False)
                pe.matmul(acc, w_hi, v_lo, start=False, stop=False)
                return pe.matmul(acc, w_lo, v_hi, start=False, stop=stop)

            def layer0(c, n, slots):
                for t in range(KT):
                    if t % 2 == 0:
                        pe.wait_ge(lo_ready, n + t // 2 + 1)
                    s = slots[t // 2]
                    mm = three_passes(acc0[:], w0_hi[:, t, :], w0_lo[:, t, :], hi[:, s, t % 2, :],
                                      lo[:, s, t % 2, :], t == 0, False)
                    if t % 2 == 1:
                        mm.then_inc(split_used, 1)
                pe.wait_ge(small_lo_ready, c + 1)
                pe.matmul(acc0[:], w16_split[:], small_split[:], start=False, stop=True).then_inc(l0_done, 1)

            pe.wait_ge(sorted_d, 2)
            for half in range(2):
                transpose_x(prod[:, half, 0, :], half)
            def ctx_share_mm(q):
                pe.matmul(prev_ps[:, q % 2, :], wt1_ctx[:, P * q:P * (q + 1)], ctx_t[:], start=True,
                          stop=True).then_inc(ctx_mm, 1)

            pe.wait_ge(tower_loaded, 16 * 6)
            ctx_share_mm(0)
            ctx_share_mm(1)
            pe.wait_ge(ctx_share_ready, 2)
            ctx_share_mm(2)
            ctx_share_mm(3)
            pe.wait_ge(summed1, 2)

            def clear_acc1(times):
                for _ in range(times):
                    clear = pe.matmul(acc1[:], identity[:], sum1[:], start=True, stop=True)
                return clear

            clear_acc1(2)
            pe.wait_ge(w_lo_ready, 3)
            layer0(0, 0, FIRST_SLOTS[:L0_PAIRS])
            clear_acc1(3)
            pe.wait_ge(l0_evacuated, 1)
            layer0(1, L0_PAIRS, FIRST_SLOTS[L0_PAIRS:])
            clear_acc1(1).then_inc(l1_cleared, 1)

            def chunk(it, par, base, last, next_bt=None):
                c = 2 * it + par
                b0 = par * (L1_PAIRS if last else PAIRS)
                pe.wait_ge(l1_evacuated, c + 1)
                for k in range(L1_PAIRS):
                    s = SLOTS[b0 + k]
                    pe.wait_ge(lo_ready, base + k + 1)
                    for u in range(2):
                        mm = three_passes(acc1[:], w1_hi[:, k, u, :], w1_lo[:, k, u, :],
                                          hi[:, s, u, :], lo[:, s, u, :], k == 0 and u == 0, False)
                    mm.then_inc(split_used, 1)
                    if k in WHOLE_AFTER:
                        m = WHOLE_AFTER.index(k)
                        pe.wait_ge(whole_ready, WHOLES * c + m + 1)
                        for u in range(2):
                            mm = pe.matmul(acc1[:], w1_whole[:, m, u, :], whole[:, m % R, u, :],
                                           start=False, stop=m == WHOLES - 1 and u == 1)
                        mm.then_inc(whole_free, 1)
                    if k == 1 and next_bt is not None:
                        pe.wait_ge(l0_evacuated, c + 2)
                        pe.wait_ge(sorted_d, next_bt + 2)
                        transpose_x(acc0, 0)
                    if k == 4 and next_bt is not None:
                        pe.wait_ge(xt_staged, 2 * next_bt + 1)
                        transpose_x(acc0, 1)
                if not last:
                    pe.wait_ge(l0_evacuated, c + 2)
                    if next_bt is not None:
                        pe.wait_ge(xt_staged, 2 * next_bt + 2)
                    layer0(c + 2, base + L1_PAIRS, SLOTS[b0 + L1_PAIRS:b0 + PAIRS])

            def two_chunks(it, next_bt=None):
                for par in range(2):
                    chunk(it, par, split_base(2 * it + par), False, next_bt if par else None)

            loop_chunks(pe, two_chunks)
            chunk(CHUNKS // 2 - 1, 0, split_base(CHUNKS - 2), True)
            chunk(CHUNKS // 2 - 1, 1, LAST_BASE, True)

            pe.wait_ge(tower_loaded, 16 * 6)
            pe.wait_ge(folded0, 2 * BT + 1)
            for q in range(H1 // P):
                pe.matmul(prod[:, q // 2, q % 2, :], wt1_sb[:, 0, P * q:P * (q + 1)], pooled0[:], start=True, stop=False)
            pe.wait_ge(folded1, 2 * BT + 2)
            for q in range(H1 // P):
                pe.matmul(prod[:, q // 2, q % 2, :], wt1_sb[:, 1, P * q:P * (q + 1)], pooled1[:, 1:BT + 1, :],
                          start=False, stop=True).then_inc(tower_mm, 1)
            for t in range(H1 // P):
                pe.wait_ge(tower_relu, t + 1)
                for q in range(H2 // P):
                    mm = pe.matmul(prev_ps[:, q, :], wt2_sb[:, t, P * q:P * (q + 1)], h1[:, t, :],
                                   start=t == 0, stop=t == H1 // P - 1)
                    if t == H1 // P - 1:
                        mm.then_inc(tower_mm, 1)
            for t in range(H2 // P):
                pe.wait_ge(tower_relu, H1 // P + t + 1)
                mm = pe.matmul(acc0[0:1, :], wt3_sb[:, t:t + 1], h2[:, t, :], start=t == 0, stop=t == H2 // P - 1)
            mm.then_inc(tower_mm, 1)


def kernel(**inputs):
    import numpy as np
    import concourse.bacc as bacc
    from concourse.bass_utils import run_bass_kernel_spmd

    nc = bacc.Bacc("TRN2", target_bir_lowering=False, num_devices=1)
    arrays = {}

    def given(name, a):
        arrays[f"in_{name}"] = np.ascontiguousarray(a)
        a = arrays[f"in_{name}"]
        return nc.dram_tensor(f"in_{name}", a.shape, mybir.dt.from_np(a.dtype), kind="ExternalInput").ap()

    n_fields = inputs["ids"].shape[1]
    scale = np.ones((P, 1), np.float32)
    scale[::4] = 0.5
    args = [given("dense_ctx", inputs["dense_ctx"]), given("ids", inputs["ids"]),
            [given(f"tbl_{f}", inputs[f"tbl_{f}"]) for f in range(n_fields)]]
    args += [given(n, inputs[n]) for n in ("W_top1", "b_top1", "W_top2", "b_top2", "W_top3",
                                           "L0_rec_filter_0", "L0_rec_filter_1")]
    args += [given("eye", np.eye(P, dtype=np.float32)), given("fold_scale", scale)]
    y = nc.dram_tensor("y", (inputs["ids"].shape[0], 1), F32, kind="ExternalOutput").ap()
    cin_tower(nc, *args, y)
    r = run_bass_kernel_spmd(nc, [arrays], core_ids=[0])
    return r.results[0]["y"]
```
